# Optimizing a Trainium2 kernel written in Bass

```python
import numpy as np
import jax
import jax.numpy as jnp

def _softmax(x, axis=-1):
    return jax.nn.softmax(x, axis=axis)

def _gelu(x):
    return jax.nn.gelu(x, approximate=True)

def _silu(x):
    return jax.nn.silu(x)

def _sigmoid(x):
    return jax.nn.sigmoid(x)

def _layernorm(x, axis=-1, eps=1e-05):
    m = jnp.mean(x, axis=axis, keepdims=True)
    v = jnp.var(x, axis=axis, keepdims=True)
    return (x - m) / jnp.sqrt(v + eps)

def _scatter_add(tgt, idx, src, axis=0):
    return tgt.at[idx].add(src)

def _segment_sum(src, seg, n):
    return jax.ops.segment_sum(src, seg, n)
kernel_name = 'mk_adaln_ffn_d1_seqx_r4_5cbd36'

def setup_inputs(seed: int=0):
    np.random.seed(seed)
    _w = jnp.asarray

    def _rec_inputs():
        import jax
        import jax.numpy as jnp
        _rk = jax.random.key(seed)
        x = 7.22e-05 + 1 * jax.random.normal(jax.random.fold_in(_rk, 1), (32, 256, 256), jnp.float32)
        _lenS = 256 - jax.random.randint(jax.random.fold_in(_rk, 7), (32,), 0, max(1, 256 // 4) + 1, jnp.int32)
        _lenS2 = 256 - jax.random.randint(jax.random.fold_in(_rk, 8), (32,), 0, max(1, 256 // 4) + 1, jnp.int32)
        cond_2048 = 0.997298 + 0.498944 * jax.random.normal(jax.random.fold_in(_rk, 11), (32, 512), jnp.float32)
        return (x, cond_2048)
    x, cond_2048 = _rec_inputs()

    def _L0_cond_setup():
        import jax, jax.numpy as jnp
        import numpy as np
        EPS_IN = 1e-05
        EPS_DM = 1e-08

        def _dcoef(weight, style):
            return jax.lax.rsqrt(jnp.einsum('oi,bi->bo', jnp.square(weight), jnp.square(style)) + EPS_DM)
        key = jax.random.key(seed)
        ks = jax.random.split(key, 7)
        B, S, H = (8, 256, 256)
        lim = 1.0 / np.sqrt(H)
        u = lambda k, shp: jax.random.uniform(k, shp, jnp.float32, -lim, lim)
        return {'x': jax.random.normal(ks[0], (B, S, H), jnp.float32), 'q_weight': u(ks[1], (H, H)), 'k_weight': u(ks[2], (H, H)), 'v_weight': u(ks[3], (H, H)), 'w_weight': u(ks[4], (H, H)), 'u_weight': u(ks[5], (H, H)), 'styles': jax.random.normal(ks[6], (B, 2 * H), jnp.float32) * 0.5 + 1.0, 'num_heads': 16}
    _L0_cond_all = _L0_cond_setup()
    _L0_cond_in = {k: v for k, v in _L0_cond_all.items() if k in ('q_weight', 'k_weight', 'v_weight', 'w_weight', 'u_weight')}
    del _L0_cond_all

    def _L0_ffn_setup():
        import math
        import jax, jax.numpy as jnp
        import numpy as np
        TOP_K = 2
        CAP_FACTOR = 1.25
        CLAMP = 10000.0
        key = jax.random.key(seed)
        k1, k2, k3, k4, k5 = jax.random.split(key, 5)
        B, S, D, F, E = (4, 512, 256, 1024, 8)
        std = 0.02
        return {'x': jax.random.normal(k1, (B, S, D), dtype=jnp.float32), 'Wr': jax.random.normal(k2, (D, E), dtype=jnp.float32) * std, 'W1': jax.random.normal(k3, (E, D, F), dtype=jnp.float32) * std, 'W3': jax.random.normal(k4, (E, D, F), dtype=jnp.float32) * std, 'W2': jax.random.normal(k5, (E, F, D), dtype=jnp.float32) * std}
    _L0_ffn_all = _L0_ffn_setup()
    _L0_ffn_in = {k: v for k, v in _L0_ffn_all.items() if k in ('Wr', 'W1', 'W3', 'W2')}
    del _L0_ffn_all
    return {'x': x, 'cond_2048': cond_2048, 'L0_cond_q_weight': _L0_cond_in['q_weight'], 'L0_cond_k_weight': _L0_cond_in['k_weight'], 'L0_cond_v_weight': _L0_cond_in['v_weight'], 'L0_cond_w_weight': _L0_cond_in['w_weight'], 'L0_cond_u_weight': _L0_cond_in['u_weight'], 'L0_ffn_Wr': _L0_ffn_in['Wr'], 'L0_ffn_W1': _L0_ffn_in['W1'], 'L0_ffn_W3': _L0_ffn_in['W3'], 'L0_ffn_W2': _L0_ffn_in['W2']}

def reference(x, cond_2048, L0_cond_q_weight, L0_cond_k_weight, L0_cond_v_weight, L0_cond_w_weight, L0_cond_u_weight, L0_ffn_Wr, L0_ffn_W1, L0_ffn_W3, L0_ffn_W2):
    import jax
    import jax.numpy as jnp

    def _L0_cond_ref(x, q_weight, k_weight, v_weight, w_weight, u_weight, styles, num_heads):
        import jax, jax.numpy as jnp
        import numpy as np
        EPS_IN = 1e-05
        EPS_DM = 1e-08

        def _dcoef(weight, style):
            return jax.lax.rsqrt(jnp.einsum('oi,bi->bo', jnp.square(weight), jnp.square(style)) + EPS_DM)
        B, S, H = x.shape
        nh = num_heads
        d = H // nh
        scale = jnp.asarray(d, x.dtype) ** (-0.5)
        s1 = styles[:, :H]
        s2 = styles[:, H:]
        x = x * s1[:, None, :]
        mu = jnp.mean(x, axis=-1, keepdims=True)
        var = jnp.mean(jnp.square(x - mu), axis=-1, keepdims=True)
        x = (x - mu) * jax.lax.rsqrt(var + EPS_IN)
        q_dc = _dcoef(q_weight, s1)
        k_dc = _dcoef(k_weight, s1)
        v_dc = _dcoef(v_weight, s1)
        w_dc = _dcoef(w_weight, s2)
        u_dc = _dcoef(u_weight, s2)

        def heads(t):
            return t.reshape(B, S, nh, d).transpose(0, 2, 1, 3)
        q = heads(jnp.einsum('bsh,oh->bso', x, q_weight) * q_dc[:, None, :])
        k = heads(jnp.einsum('bsh,oh->bso', x, k_weight) * k_dc[:, None, :])
        v_flat = jnp.einsum('bsh,oh->bso', x, v_weight) * v_dc[:, None, :] * s2[:, None, :]
        skip = v_flat
        v = heads(v_flat)
        attn = jnp.einsum('bhqd,bhkd->bhqk', q, k) * scale
        attn = jax.nn.softmax(attn, axis=-1)
        out = jnp.einsum('bhqk,bhkd->bhqd', attn, v).transpose(0, 2, 1, 3).reshape(B, S, H)
        out = jnp.einsum('bsh,oh->bso', out, w_weight) * w_dc[:, None, :]
        skip = jnp.einsum('bsh,oh->bso', skip, u_weight) * u_dc[:, None, :]
        return out + skip

    def _L0_ffn_ref(x, Wr, W1, W3, W2):
        import math
        import jax, jax.numpy as jnp
        import numpy as np
        TOP_K = 2
        CAP_FACTOR = 1.25
        CLAMP = 10000.0
        B, S, D = x.shape
        E = Wr.shape[1]
        K = TOP_K
        T = B * S
        cap = max(1, math.ceil(T * K * CAP_FACTOR / E))
        xf = x.reshape(T, D)
        logits = jnp.clip(xf @ Wr, -CLAMP, CLAMP)
        top_v, top_i = jax.lax.top_k(logits, K)
        m = jnp.max(top_v, axis=-1, keepdims=True)
        expv = jnp.exp(top_v - m)
        top_p = expv / (jnp.sum(expv, axis=-1, keepdims=True) + 1e-12)
        Sp = T * K
        experts = top_i.reshape(Sp)
        weights = top_p.reshape(Sp)
        tokens = jnp.repeat(jnp.arange(T), K)
        oh = experts[:, None] == jnp.arange(E)[None, :]
        pos = jnp.sum(jnp.cumsum(oh.astype(jnp.int32), axis=0) * oh, axis=-1) - 1
        kept = pos < cap
        pos_safe = jnp.where(kept, pos, cap)
        xe = jnp.zeros((E, cap + 1, D), x.dtype).at[experts, pos_safe].set(xf[tokens])[:, :cap]
        h = jax.nn.silu(jnp.einsum('ecd,edf->ecf', xe, W1)) * jnp.einsum('ecd,edf->ecf', xe, W3)
        ye = jnp.einsum('ecf,efd->ecd', h, W2)
        yp = ye[experts, jnp.minimum(pos_safe, cap - 1)]
        wk = weights * kept.astype(weights.dtype)
        out = jnp.zeros((T, D), x.dtype).at[tokens].add(wk[:, None] * yp)
        return out.reshape(B, S, D)
    x = x + _L0_ffn_ref(_L0_cond_ref(x, L0_cond_q_weight, L0_cond_k_weight, L0_cond_v_weight, L0_cond_w_weight, L0_cond_u_weight, cond_2048, 16), L0_ffn_Wr, L0_ffn_W1, L0_ffn_W3, L0_ffn_W2)
    return x

_drawn_inputs = setup_inputs


def setup_inputs(seed=0):
    import zlib

    import numpy as np

    out = dict(_drawn_inputs(seed))
    spreads = {}
    factors = {'cond_2048': 3.212,
     'L0_cond_q_weight': 8.0,
     'L0_cond_k_weight': 8.0,
     'L0_cond_v_weight': 2.832,
     'L0_cond_w_weight': 8.0,
     'L0_cond_u_weight': 2.82,
     'L0_ffn_Wr': 3.292,
     'L0_ffn_W1': 2.853,
     'L0_ffn_W3': 2.825,
     'L0_ffn_W2': 2.822}
    for name, (base, spread) in spreads.items():
        noise = np.random.default_rng([zlib.crc32(name.encode()), seed]).standard_normal(out[name].shape)
        drawn = base * np.exp(spread * noise) if base else spread * noise
        out[name] = jnp.asarray(drawn.astype(out[name].dtype))
    for name, factor in factors.items():
        out[name] = (out[name] * factor).astype(out[name].dtype)
    return out
```

```python
from contextlib import ExitStack

import concourse.bass as bass
from concourse import mybir

ALU = mybir.AluOpType
ACT = mybir.ActivationFunctionType
AX = mybir.AxisListType
F32 = mybir.dt.float32
BF16 = mybir.dt.bfloat16
I32 = mybir.dt.int32
U32 = mybir.dt.uint32

P = 128
B, S, D = 32, 256, 256
H, HD = 16, 16
NE, F, TOPK = 8, 1024, 2
T = B * S
CAP = -(-T * TOPK * 5 // (4 * NE))
C = D // P
FC = F // P
BLK = 512
JT = BLK // P
NBLK = CAP // BLK
assert NBLK * BLK == CAP and S == D == C * P
CLAMP = 10000.0
FAR = 65536.0
Q_PARTS = (0, 0, 1, 0, 2, 1)
K_PARTS = (0, 1, 0, 2, 0, 1)
KS = HD * len(Q_PARTS)
KM = KS + 3
VW = 32

BANK = {"maxT": 1, "o2a": 0, "o2b": 1, "xT": 0, "oT": 1, "q": 0, "w": 1, "u": 0,
        "k": 1, "y": 0, "lg": 1, "vT": 0, "v": 1, "rt": 0}
A_USES = ("xT", "q", "k", "vT", "v")
SLOT_USES = ("maxT", "o2a", "o2b", "xT", "oT", "q", "w", "u", "k", "y", "lg", "vT", "v", "rt")


def bank_counts():
    n, at = [0, 0], {}

    def use(name, t):
        n[BANK[name]] += 1
        at[name, t] = n[BANK[name]]

    for t in (0, 1):
        for u in A_USES:
            use(u, t)
    use("maxT", 0)
    for s in range(B):
        for u in SLOT_USES:
            t = s + 2 if u in A_USES else s + 1 if u == "maxT" else s
            if t < B:
                use(u, t)
    return at, n


COUNTS, BANK_TOTAL = bank_counts()


class Count:

    def __init__(self, first, step=0, i=None):
        self.first, self.step, self.i = first, step, i

    def __add__(self, n):
        return Count(self.first + n, self.step, self.i)

    def __sub__(self, n):
        return self + -n

    def __mul__(self, n):
        return Count(self.first * n, self.step * n, self.i)

    @property
    def value(self):
        return max(self.first, 0) if self.i is None else self.i * self.step + self.first


def uses(name, t):
    if t.i is None:
        return Count(COUNTS[name, t.first])
    ahead = COUNTS[name, t.first + t.step] - COUNTS[name, t.first]
    assert ahead == COUNTS[name, t.first + 2 * t.step] - COUNTS[name, t.first + t.step]
    return Count(COUNTS[name, t.first], ahead, t.i)


def ahead(eng, count):
    return count.value if count.i is None else eng.compute_val(count.value)


def adaln_moe(nc, x, cond, wq, wk, wv, ww, wu, wr, w1, w3, w2, out):
    with ExitStack() as ctx:
        def sb(name, shape, dt=F32):
            return ctx.enter_context(nc.sbuf_tensor(name, shape, dt))

        def pb(name):
            return ctx.enter_context(nc.psum_tensor(name, [P, 512], F32))

        def sem(name):
            return ctx.enter_context(nc.semaphore(name))

        y_rows = nc.dram_tensor("y_rows", [T, D], F32, kind="Internal").ap()
        slots = nc.dram_tensor("slot_table", [NE * CAP, 2], I32, kind="Internal").ap()
        parts_rows = nc.dram_tensor("parts_rows", [2, 2, 3, D, S], BF16, kind="Internal").ap()
        x_rows = x.rearrange("b s d -> (b s) d")
        out_rows = out.rearrange("b s d -> (b s) d")

        ident = sb("ident", [P, P])
        before = sb("before", [P, P], BF16)
        ones = sb("ones", [P, P], BF16)
        expert_no = sb("expert_no", [P, NE])
        expert_no_i = sb("expert_no_i", [P, NE], I32)
        expert_base = sb("expert_base", [P, NE])
        token_no = sb("token_no", [P, C], I32)
        token_f = sb("token_f", [P, C])
        empty = sb("empty", [P, NE * CAP // P, 2], I32)
        wT = [sb(f"wT{n}", [P, C, D]) for n in range(5)]
        wr_sb = sb("wr_sb", [P, C, NE])
        cond_sb = sb("cond_sb", [B, 2 * D])
        condT = sb("condT", [P, 4, B])
        condsq = sb("condsq", [P, 4, B])
        dcoef = [sb(f"dcoef{n}", [P, C, B]) for n in range(5)]
        x_tok = [sb(f"x_tok{p}", [P, C, D]) for p in (0, 1)]
        s1_all = [sb(f"s1_all{p}", [P, D]) for p in (0, 1)]
        xs = sb("xs", [P, C, D])
        stats = sb("stats", [P, C, 6])
        mv = sb("mv", [P, C, 2])
        var = sb("var", [P, C])
        rstd = sb("rstd", [P, C])
        minus_half = sb("minus_half", [P, C * B])
        xn = sb("xn", [P, C, D])
        xT = sb("xT", [P, C, S])
        qparts = sb("qparts", [P, 3, C, S], BF16)
        kparts = sb("kparts", [P, 3, C, S], BF16)
        qrest = sb("qrest", [P, C, S])
        krest = sb("krest", [P, C, S])
        vT = [sb(f"vT{p}", [P, C, S]) for p in (0, 1)]
        vaug = [sb(f"vaug{p}", [P, C, H, VW]) for p in (0, 1)]
        qst = [sb(f"qst{p}", [P, H, S], BF16) for p in (0, 1)]
        kst = [sb(f"kst{p}", [P, H, S], BF16) for p in (0, 1)]
        mx = sb("mx", [P, C, H])
        nm = sb("nm", [H, 3, S], BF16)
        nrest = sb("nrest", [H, S])
        probs = [sb(f"probs{n}", [P, C, S]) for n in range(8)]
        wload = probs
        oTa = sb("oTa", [P, 4, S])
        rden = sb("rden", [P, C, H])
        on = sb("on", [P, C, D])
        oT = sb("oT", [P, C, S])
        skipT = sb("skipT", [P, C, S])
        yT = sb("yT", [P, C, S])
        y_tok = sb("y_tok", [P, C, D])
        lg = sb("lg", [P, C, NE])
        top8 = sb("top8", [P, C, 8])
        idx8 = sb("idx8", [P, C, 8], U32)
        idxf = sb("idxf", [P, C, TOPK])
        onehot = sb("onehot", [P, C, TOPK, NE])
        chosen = sb("chosen", [P, C, NE], BF16)
        gap = sb("gap", [P, C])
        ex = sb("ex", [P, C])
        den = sb("den", [P, C])
        pr = sb("pr", [P, C, TOPK])
        base = sb("base", [P, C + 1, NE])
        pos = sb("pos", [P, C, NE])
        over = sb("over", [P, C, NE])
        place = sb("place", [P, C, NE])
        picked = sb("picked", [P, C, TOPK, NE])
        slot_f = sb("slot_f", [P, C, TOPK])
        slot_i = sb("slot_i", [P, C, TOPK], U32)
        entry = sb("entry", [P, C, TOPK, 2], I32)
        w1_sb = [sb(f"w1_sb{p}", [P, C, F]) for p in (0, 1)]
        w3_sb = [sb(f"w3_sb{p}", [P, C, F]) for p in (0, 1)]
        w2_sb = [sb(f"w2_sb{p}", [P, FC, D]) for p in (0, 1)]
        tab = [sb(f"tab{p}", [P, JT, 2], I32) for p in (0, 1)]

        banks = [pb(f"bank{n}") for n in range(8)]
        gen = banks[0:2]
        sc_ps = banks[2:4]
        st_ps = banks[4:6]
        o_ps = banks[6:8]
        gen3 = [g[:, :].rearrange("p (c n) -> p c n", c=C) for g in gen]

        filled = [sem(f"bank{n}_filled") for n in (0, 1)]
        drained = [sem(f"bank{n}_drained") for n in (0, 1)]
        w_in = sem("w_in")
        small_in = sem("small_in")
        const_ready = sem("const_ready")
        const_step = sem("const_step")
        set_filled = sem("set_filled")
        set_drained = sem("set_drained")
        sq_ready = sem("sq_ready")
        numbers_ready = sem("numbers_ready")
        roots_ready = sem("roots_ready")
        d_ready = sem("d_ready")
        table_empty = sem("table_empty")
        out_is_x = sem("out_is_x")
        x_in = [sem(f"x_in{p}") for p in (0, 1)]
        xs_ready = sem("xs_ready")
        stats_ready = sem("stats_ready")
        aggr_ready = sem("aggr_ready")
        var_ready = sem("var_ready")
        rstd_ready = sem("rstd_ready")
        xn_ready = sem("xn_ready")
        q1_ready = sem("q1_ready")
        k1_ready = sem("k1_ready")
        q2_ready = sem("q2_ready")
        k2_ready = sem("k2_ready")
        q3_ready = sem("q3_ready")
        k3_ready = sem("k3_ready")
        parts_out = sem("parts_out")
        stack_in = [sem(f"stack_in{p}") for p in (0, 1)]
        s_filled = sem("s_filled")
        s_drained = sem("s_drained")
        n1_ready = sem("n1_ready")
        n2_ready = sem("n2_ready")
        n3_ready = sem("n3_ready")
        nm_in = sem("nm_in")
        t_filled = sem("t_filled")
        p_ready = sem("p_ready")
        av_done = sem("av_done")
        o_drained = sem("o_drained")
        rden_ready = sem("rden_ready")
        y_out = sem("y_out")
        top_ready = sem("top_ready")
        idx_ready = sem("idx_ready")
        idxf_ready = sem("idxf_ready")
        onehot_ready = sem("onehot_ready")
        chosen_ready = sem("chosen_ready")
        gap_ready = sem("gap_ready")
        ex_ready = sem("ex_ready")
        den_ready = sem("den_ready")
        pr_ready = sem("pr_ready")
        base_step = sem("base_step")
        pos_ready = sem("pos_ready")
        over_ready = sem("over_ready")
        place_step = sem("place_step")
        picked_ready = sem("picked_ready")
        slotf_ready = sem("slotf_ready")
        token_read = sem("token_read")
        entry_ready = sem("entry_ready")
        entries_out = sem("entries_out")
        wexp_in = [sem(f"wexp_in{p}") for p in (0, 1)]
        tab_in = sem("tab_in")
        xe_zero = sem("xe_zero")
        xe_in = [sem(f"xe_in{p}") for p in (0, 1)]
        xeT_filled = sem("xeT_filled")
        xeT_ready = sem("xeT_ready")
        up_filled = sem("up_filled")
        sg_ready = sem("sg_ready")
        h_ready = sem("h_ready")
        down_filled = sem("down_filled")
        ye_act = sem("ye_act")
        ye_dve = sem("ye_dve")
        adds_out = sem("adds_out")

        weights = (wq, wk, wv, ww, wu)
        WQ, WK, WV, WW, WU = range(5)

        xe = [sb(f"xe{p}", [P, JT, D]) for p in (0, 1)]
        xeT = sb("xeT", [P, C, BLK])
        sg = [sb(f"sg{p}", [P, BLK]) for p in (0, 1)]
        hid = sb("hid", [P, FC, BLK])
        ye = sb("ye", [P, JT, D])
        squares = [probs[5], probs[6], probs[7], xn, on]

        block = ctx.enter_context(nc.Block())

        def at(i, j):
            return Count(i * 2 * NBLK + j) if isinstance(i, int) else Count(j, 2 * NBLK, i)

        def last_one(i, j):
            return isinstance(i, int) and j == 2 * NBLK - 1

        def slots_of(eng, pro, slot, last):
            pro()
            for p in (0, 1):
                slot(Count(p), p, True)
            with eng.Fori(1, B // 2 - 1) as i:
                for p in (0, 1):
                    slot(Count(p, 2, i), p, True)
            for p in (0, 1):
                slot(Count(B - 2 + p), p, False)
            last()

        @block.sync
        def _(sp):
            for n, w in enumerate(weights):
                sp.dma_start(wload[n][:, :, :], w.rearrange("(c p) i -> p c i", p=P)).then_inc(w_in, 16)
            sp.dma_start(cond_sb[:, :], cond).then_inc(small_in, 16)
            sp.dma_start(wr_sb[:, :, :], wr.rearrange("(c p) e -> p c e", p=P)).then_inc(small_in, 16)

            def load_x(t, p):
                met = ahead(sp, t - 1)
                sp.wait_ge(const_ready, 12)
                sp.wait_ge(xs_ready, met)
                sp.dma_start(x_tok[p][:, :, :], x[bass.ds(t.value, 1), :, :].rearrange("b (c p) d -> p (b c) d", p=P))\
                    .then_inc(x_in[p], 16)
                sp.dma_start(s1_all[p][:, :], cond[bass.ds(t.value, 1), 0:D].to_broadcast([P, D])).then_inc(x_in[p], 16)

            def stack(t, p):
                for parts, st, first, third, n0, order in (
                        (qparts, qst, q1_ready, q3_ready, 1, Q_PARTS), (kparts, kst, k1_ready, k3_ready, 2, K_PARTS)):
                    sp.wait_ge(first, (t + 1).value)
                    sp.wait_ge(third, (t + 1).value)
                    sp.dma_start(parts_rows[n0 - 1, p].rearrange("n (c p) s -> p n c s", p=P), parts[:, :, :, :])\
                        .then_inc(parts_out, 16)
                    met = ahead(sp, t * 32 + 16 * n0)
                    sp.wait_ge(const_ready, 12)
                    sp.wait_ge(parts_out, met)
                    sp.wait_ge(t_filled, ((t - 1) * H).value)
                    for n, part in enumerate(order):
                        sp.dma_start(st[p][n * HD:(n + 1) * HD, :, :],
                                     parts_rows[n0 - 1, p, part].rearrange("(h d) s -> d h s", d=HD))\
                            .then_inc(stack_in[p], 16)

            def max_rows(t, p):
                met = ahead(sp, t + 1)
                sp.wait_ge(const_ready, 12)
                sp.wait_ge(n3_ready, met)
                sp.wait_ge(t_filled, ((t - 1) * H).value)
                for n in range(3):
                    sp.dma_start(qst[p][KS + n:KS + n + 1, :, :], nm[:, n, :]).then_inc(nm_in, 16)

            def store_y(t, p):
                met = ahead(sp, uses("y", t))
                sp.wait_ge(const_ready, 12)
                sp.wait_ge(drained[BANK["y"]], met)
                sp.dma_start(y_rows[bass.ds((t * S).value, S), :].rearrange("(c p) d -> p c d", p=P), y_tok[:, :, :])\
                    .then_inc(y_out, 16)

            def load_expert(e, p):
                for dst, src in ((w1_sb, w1), (w3_sb, w3)):
                    sp.dma_start(dst[p][:, :, :], src[bass.ds(e.value, 1), :, :].rearrange("e (c p) f -> p (e c) f", p=P))\
                        .then_inc(wexp_in[p], 16)
                sp.dma_start(w2_sb[p][:, :, :], w2[bass.ds(e.value, 1), :, :].rearrange("e (c p) d -> p (e c) d", p=P))\
                    .then_inc(wexp_in[p], 16)

            def pro():
                load_x(Count(0), 0)
                load_x(Count(1), 1)
                sp.dma_start(out_rows.rearrange("(p n) d -> p (n d)", p=P),
                             x_rows.rearrange("(p n) d -> p (n d)", p=P)).then_inc(out_is_x, 16)
                for p in (0, 1):
                    load_expert(Count(p), p)
                stack(Count(0), 0)
                max_rows(Count(0), 0)
                stack(Count(1), 1)

            def slot(s, p, more):
                if more:
                    load_x(s + 2, p)
                if more or p == 0:
                    max_rows(s + 1, 1 - p)
                if more:
                    stack(s + 2, p)
                store_y(s, p)

            def last():
                with sp.Fori(1, NE // 2) as i:
                    for p in (0, 1):
                        met = ahead(sp, Count((p - 1) * 2 * NBLK, 4 * NBLK, i))
                        sp.wait_ge(const_ready, 12)
                        sp.wait_ge(down_filled, met)
                        load_expert(Count(p, 2, i), p)

            slots_of(sp, pro, slot, last)
            sp.wait_ge(adds_out, NE * NBLK * JT * 16)
            sp.wait_ge(y_out, B * 16)

        @block.gpsimd
        def _(pool):
            pool.memset(ident[:, :], 0.0).then_inc(const_step, 1)
            pool.memset(before[:, :], 1.0).then_inc(const_step, 1)
            pool.wait_ge(const_step, 2)
            pool.affine_select(out=ident[:, :], in_=ident[:, :], compare_op=ALU.not_equal, fill=1.0, base=0,
                               pattern=[[-1, P]], channel_multiplier=1).then_inc(const_ready, 1)
            pool.affine_select(out=before[:, :], in_=before[:, :], compare_op=ALU.is_gt, fill=0.0, base=0,
                               pattern=[[1, P]], channel_multiplier=-1).then_inc(const_ready, 1)
            pool.memset(ones[:, :], 1.0).then_inc(const_ready, 1)
            pool.memset(minus_half[:, :], -0.5).then_inc(const_ready, 1)
            pool.iota(expert_no_i[:, :], pattern=[[1, NE]], base=0, channel_multiplier=0).then_inc(const_ready, 1)
            pool.iota(token_no[:, :], pattern=[[P, C]], base=0, channel_multiplier=1).then_inc(const_ready, 1)
            for p in (0, 1):
                pool.memset(vaug[p][:, :, :, :], 0.0).then_inc(const_step, 1)
                pool.memset(xe[p][:, :, :], 0.0).then_inc(xe_zero, 1)
            pool.memset(empty[:, :, 0], T).then_inc(const_ready, 1)
            pool.memset(empty[:, :, 1], 0).then_inc(const_ready, 1)
            pool.wait_ge(const_step, 4)
            for p in (0, 1):
                pool.memset(vaug[p][:, :, :, HD:HD + 1], 1.0).then_inc(const_ready, 1)
            pool.wait_ge(const_ready, 12)
            pool.dma_start(slots.rearrange("(p n) w -> p (n w)", p=P), empty[:, :, :].rearrange("p n w -> p (n w)"))\
                .then_inc(table_empty, 16)

            for n in range(5):
                pool.wait_ge(set_drained, n + 7)
                pool.tensor_tensor(dcoef[n][:, :, :], dcoef[n][:, :, :],
                                   minus_half[:, :].rearrange("p (c b) -> p c b", c=C), ALU.pow)\
                    .then_inc(roots_ready, 1)

            def scale_x(t, p):
                pool.wait_ge(x_in[p], (t * 16 + (32 - 16 * p)).value)
                pool.wait_ge(xn_ready, t.value)
                pool.tensor_tensor(xs[:, :, :], x_tok[p][:, :, :],
                                   s1_all[p][:, :].unsqueeze(1).to_broadcast([P, C, D]), ALU.mult)\
                    .then_inc(xs_ready, 1)

            def inverse_root(t):
                pool.wait_ge(var_ready, (t + 1).value)
                pool.tensor_tensor(rstd[:, :], var[:, :], minus_half[:, 0:C], ALU.pow).then_inc(rstd_ready, 1)

            def small_parts(t, use, parts, rest, second, third):
                met = ahead(pool, uses(use, t))
                pool.wait_ge(const_ready, 12)
                pool.wait_ge(drained[BANK[use]], met)
                pool.tensor_copy(parts[:, 1, :, :], rest[:, :, :]).then_inc(second, 1)
                pool.wait_ge(second, (t + 1).value)
                pool.tensor_tensor(parts[:, 2, :, :], rest[:, :, :], parts[:, 1, :, :], ALU.subtract)\
                    .then_inc(third, 1)

            def split(t, p):
                small_parts(t, "q", qparts, qrest, q2_ready, q3_ready)
                small_parts(t, "k", kparts, krest, k2_ready, k3_ready)

            def enter(t, p):
                met = ahead(pool, t + 1)
                pool.wait_ge(const_ready, 12)
                pool.wait_ge(entry_ready, met)
                for c in range(C):
                    for k in range(TOPK):
                        pool.indirect_dma_start(
                            out=slots, out_offset=bass.IndirectOffsetOnAxis(ap=slot_i[:, c, k:k + 1], axis=0),
                            in_=entry[:, c, k, :], in_offset=None, bounds_check=NE * CAP - 1, oob_is_err=False)\
                            .then_inc(entries_out, 16)

            def pro():
                for t, p in ((Count(0), 0), (Count(1), 1)):
                    scale_x(t, p)
                    inverse_root(t)
                    split(t, p)
                pool.wait_ge(table_empty, 16)

            def slot(s, p, more):
                if more:
                    scale_x(s + 2, p)
                    inverse_root(s + 2)
                    split(s + 2, p)
                enter(s, p)

            def fetch(nb, b):
                pool.dma_start(tab[b][:, :, :], slots[bass.ds((nb * BLK).value, BLK), :].rearrange("(p j) w -> p j w", j=JT))\
                    .then_inc(tab_in, 16)
                met = ahead(pool, nb * 16 + 16)
                pool.wait_ge(const_ready, 12)
                pool.wait_ge(tab_in, met)
                for j in range(JT):
                    pool.indirect_dma_start(
                        out=xe[b][:, j, :], out_offset=None, in_=y_rows,
                        in_offset=bass.IndirectOffsetOnAxis(ap=tab[b][:, j, 0:1].bitcast(U32), axis=0),
                        bounds_check=T - 1, oob_is_err=False).then_inc(xe_in[b], 16)

            def add(nb, b):
                met = ahead(pool, nb + 1)
                pool.wait_ge(const_ready, 12)
                pool.wait_ge(ye_act, met)
                pool.wait_ge(ye_dve, (nb + 1).value)
                for j in range(JT):
                    pool.indirect_dma_start(
                        out=out_rows, out_offset=bass.IndirectOffsetOnAxis(ap=tab[b][:, j, 0:1].bitcast(U32), axis=0),
                        in_=ye[:, j, :], in_offset=None, bounds_check=T - 1, oob_is_err=False,
                        compute_op=ALU.add).then_inc(adds_out, 16)

            def last():
                pool.wait_ge(entries_out, B * C * TOPK * 16)
                pool.wait_ge(y_out, B * 16)
                pool.wait_ge(xe_zero, 2)
                pool.wait_ge(out_is_x, 16)
                fetch(Count(0), 0)

                def blocks(i, more):
                    for j in range(2 * NBLK):
                        if more or j < 2 * NBLK - 1:
                            fetch(at(i, j + 1), (j + 1) % 2)
                        add(at(i, j), j % 2)
                        met = ahead(pool, (at(i, j) + 1) * (JT * 16))
                        pool.wait_ge(const_ready, 12)
                        pool.wait_ge(adds_out, met)

                with pool.Fori(0, NE // 2 - 1) as i:
                    blocks(i, True)
                blocks(NE // 2 - 1, False)

            slots_of(pool, pro, slot, last)

        @block.scalar
        def _(act):
            act.wait_ge(d_ready, 3)

            def ev_xT(t, p):
                b = BANK["xT"]
                act.wait_ge(filled[b], uses("xT", t).value)
                act.activation(xT[:, :, :], gen3[b], ACT.Copy).then_inc(drained[b], 1)

            def first_part(t, p, use, n, parts, first):
                b = BANK[use]
                act.wait_ge(filled[b], uses(use, t).value)
                for c in range(C):
                    ins = act.activation(parts[:, 0, c, :], gen3[b][:, c, :], ACT.Copy,
                                         scale=dcoef[n][:, c, bass.ds(t.value, 1)])
                ins.then_inc(first, 1)

            def parts_free(t, n):
                act.wait_ge(parts_out, (t * 32 - (32 - 16 * n)).value)

            def ev_vT(t, p):
                b = BANK["vT"]
                act.wait_ge(filled[b], uses("vT", t).value)
                for c in range(C):
                    ins = act.activation(vT[p][:, c, :], gen3[b][:, c, :], ACT.Copy,
                                         scale=dcoef[WV][:, c, bass.ds(t.value, 1)])
                ins.then_inc(drained[b], 1)

            def exps(t, p, g):
                if g >= 2:
                    act.wait_ge(av_done, (t * 4 + (g - 1)).value)
                for h in range(4 * g, 4 * g + 4):
                    act.wait_ge(t_filled, (t * H + (h + 1)).value)
                    act.activation(probs[h % 8][:, :, :], st_ps[h % 2][:, :].rearrange("p (c q) -> p c q", c=C),
                                   ACT.Exp).then_inc(p_ready, 1)

            def ev_o(t, p, n):
                act.wait_ge(av_done, (t * 4 + (2 * n + 2)).value)
                act.activation(oTa[:, 2 * n:2 * n + 2, :], o_ps[n][:, :].rearrange("p (g q) -> p g q", g=2), ACT.Copy)\
                    .then_inc(o_drained, 1)

            def ev_oT(t, p):
                b = BANK["oT"]
                act.wait_ge(filled[b], uses("oT", t).value)
                act.activation(oT[:, :, :], gen3[b], ACT.Copy).then_inc(drained[b], 1)

            def ev_u(t, p):
                b = BANK["u"]
                act.wait_ge(filled[b], uses("u", t).value)
                for c in range(C):
                    ins = act.activation(skipT[:, c, :], gen3[b][:, c, :], ACT.Copy,
                                         scale=dcoef[WU][:, c, bass.ds(t.value, 1)])
                ins.then_inc(drained[b], 1)

            def ev_y(t, p):
                b = BANK["y"]
                act.wait_ge(y_out, (t * 16).value)
                act.wait_ge(filled[b], uses("y", t).value)
                act.activation(y_tok[:, :, :], gen3[b], ACT.Copy).then_inc(drained[b], 1)

            def ex_gap(t, p):
                act.wait_ge(gap_ready, (t + 1).value)
                act.wait_ge(pr_ready, t.value)
                act.activation(ex[:, :], gap[:, :], ACT.Exp).then_inc(ex_ready, 1)

            def pro():
                for t, p in ((Count(0), 0), (Count(1), 1)):
                    ev_xT(t, p)
                    parts_free(t, 1)
                    first_part(t, p, "q", WQ, qparts, q1_ready)
                    parts_free(t, 2)
                    first_part(t, p, "k", WK, kparts, k1_ready)
                    ev_vT(t, p)

            def slot(s, p, more):
                for g in range(4):
                    exps(s, p, g)
                    if g == 3:
                        ev_o(s, p, 0)
                ev_o(s, p, 1)
                if more:
                    ev_xT(s + 2, p)
                ev_oT(s, p)
                if more:
                    parts_free(s + 2, 1)
                    first_part(s + 2, p, "q", WQ, qparts, q1_ready)
                ev_u(s, p)
                if more:
                    parts_free(s + 2, 2)
                    first_part(s + 2, p, "k", WK, kparts, k1_ready)
                ev_y(s, p)
                ex_gap(s, p)
                if more:
                    ev_vT(s + 2, p)

            def blocks(i):
                for j in range(2 * NBLK):
                    nb = at(i, j)
                    for f in range(FC):
                        act.wait_ge(up_filled, (nb * FC + (f + 1)).value)
                        act.activation(sg[f % 2][:, :], banks[2 + f % 2][:, :], ACT.Silu).then_inc(sg_ready, 1)
                    act.wait_ge(down_filled, (nb * 2 + 2).value)
                    if last_one(i, j):
                        act.wait_ge(adds_out, (nb * (JT * 16)).value)
                    for tt in (2, 3):
                        ins = act.activation(ye[:, tt, :], o_ps[1][:, (tt - 2) * D:(tt - 1) * D], ACT.Copy,
                                             scale=tab[j % 2][:, tt, 1:2].bitcast(F32))
                    ins.then_inc(ye_act, 1)

            def last():
                with act.Fori(0, NE // 2 - 1) as i:
                    blocks(i)
                blocks(NE // 2 - 1)

            slots_of(act, pro, slot, last)

        @block.vector
        def _(dve):
            for p in (0, 1):
                dve.memset(kst[p][KS:KM, :, :], 1.0).then_inc(const_ready, 1)
            dve.wait_ge(const_ready, 12)
            dve.tensor_copy(expert_no[:, :], expert_no_i[:, :]).then_inc(numbers_ready, 1)
            dve.tensor_copy(token_f[:, :], token_no[:, :]).then_inc(numbers_ready, 1)
            dve.memset(base[:, 0, :], 0.0).then_inc(base_step, 1)
            dve.wait_ge(numbers_ready, 2)
            dve.tensor_scalar(expert_base[:, :], expert_no[:, :], float(CAP), None, ALU.mult).then_inc(d_ready, 1)
            dve.wait_ge(set_filled, 1)
            dve.tensor_copy(condT[:, :, :], banks[2][:, 0:4 * B].rearrange("p (c b) -> p c b", c=4))\
                .then_inc(set_drained, 1)
            dve.wait_ge(set_drained, 1)
            dve.tensor_tensor(condsq[:, :, :], condT[:, :, :], condT[:, :, :], ALU.mult).then_inc(sq_ready, 1)
            for n in range(5):
                dve.wait_ge(set_filled, n + 2)
                dve.tensor_copy(wT[n][:, :, :], banks[2 + (n + 1) % 2][:, :].rearrange("p (c o) -> p c o", c=C))\
                    .then_inc(set_drained, 1)
                dve.wait_ge(set_drained, n + 2)
                dve.tensor_tensor(squares[n][:, :, :], wT[n][:, :, :], wT[n][:, :, :], ALU.mult).then_inc(sq_ready, 1)
            for n in range(5):
                dve.wait_ge(set_filled, n + 7)
                ps = banks[2 + n % 2][:, 0:C * B].rearrange("p (c b) -> p c b", c=C)
                dve.tensor_scalar(dcoef[n][:, :, :], ps, 1e-8, None, ALU.add).then_inc(set_drained, 1)
            dve.wait_ge(roots_ready, 5)
            dve.tensor_scalar(dcoef[WQ][:, :, :], dcoef[WQ][:, :, :], HD ** -0.5, None, ALU.mult).then_inc(d_ready, 1)
            dve.tensor_tensor(dcoef[WV][:, :, :], dcoef[WV][:, :, :], condT[:, C:2 * C, :], ALU.mult)\
                .then_inc(d_ready, 1)
            dve.wait_ge(d_ready, 3)

            def norm(t, p):
                dve.wait_ge(xs_ready, (t + 1).value)
                for c in range(C):
                    ins = dve.bn_stats(stats[:, c, :], xs[:, c, :])
                ins.then_inc(stats_ready, 1)
                met = ahead(dve, t + 1)
                dve.wait_ge(const_ready, 12)
                dve.wait_ge(stats_ready, met)
                for c in range(C):
                    ins = dve.bn_aggr(mv[:, c, :], stats[:, c, :])
                ins.then_inc(aggr_ready, 1)
                dve.wait_ge(aggr_ready, (t + 1).value)
                dve.tensor_scalar(var[:, :], mv[:, :, 1], 1e-5, None, ALU.add).then_inc(var_ready, 1)
                dve.wait_ge(rstd_ready, (t + 1).value)
                for c in range(C):
                    ins = dve.tensor_scalar(xn[:, c, :], xs[:, c, :], mv[:, c, 0:1], rstd[:, c:c + 1],
                                            ALU.subtract, ALU.mult)
                ins.then_inc(xn_ready, 1)

            def rest(t, p, use, n, parts, rst, first, third):
                b = BANK[use]
                dve.wait_ge(first, (t + 1).value)
                dve.wait_ge(third, t.value)
                for c in range(C):
                    ins = dve.scalar_tensor_tensor(out=rst[:, c, :], in0=gen3[b][:, c, :],
                                                   scalar=dcoef[n][:, c, bass.ds(t.value, 1)], in1=parts[:, 0, c, :],
                                                   op0=ALU.mult, op1=ALU.subtract)
                ins.then_inc(drained[b], 1)

            def ev_v(t, p):
                b = BANK["v"]
                dve.wait_ge(av_done, ((t - 1) * 4).value)
                dve.wait_ge(filled[b], uses("v", t).value)
                for c in range(C):
                    ins = dve.tensor_copy(vaug[p][:, c, :, 0:HD], gen3[b][:, c, :].rearrange("p (h d) -> p h d", d=HD))
                ins.then_inc(drained[b], 1)

            def maxima(t, p, g):
                for h in range(4 * g, 4 * g + 4):
                    dve.wait_ge(s_filled, (t * H + (h + 1)).value)
                    dve.tensor_reduce(mx[:, :, h], sc_ps[h % 2][:, :].rearrange("p (c k) -> p c k", c=C), AX.X, ALU.max)\
                        .then_inc(s_drained, 1)

            def minus_max(t, p):
                b = BANK["maxT"]
                ps = gen[b][0:H, 0:S]
                dve.wait_ge(nm_in, (t * 48).value)
                dve.wait_ge(filled[b], uses("maxT", t).value)
                dve.tensor_scalar(nm[:, 0, :], ps, -1.0, None, ALU.mult).then_inc(n1_ready, 1)
                dve.wait_ge(n1_ready, (t + 1).value)
                dve.scalar_tensor_tensor(out=nrest[:, :], in0=ps, scalar=-1.0, in1=nm[:, 0, :],
                                         op0=ALU.mult, op1=ALU.subtract).then_inc(drained[b], 1)
                dve.wait_ge(drained[b], uses("maxT", t).value)
                dve.tensor_copy(nm[:, 1, :], nrest[:, :]).then_inc(n2_ready, 1)
                dve.wait_ge(n2_ready, (t + 1).value)
                dve.tensor_tensor(nm[:, 2, :], nrest[:, :], nm[:, 1, :], ALU.subtract).then_inc(n3_ready, 1)

            def normalise(t, p, c):
                use = ("o2a", "o2b")[c]
                b = BANK[use]
                ps = gen[b][:, :].rearrange("p (h w) -> p h w", w=VW)
                dve.wait_ge(filled[b], uses(use, t).value)
                dve.reciprocal(rden[:, c, :], ps[:, :, HD]).then_inc(rden_ready, 1)
                dve.wait_ge(rden_ready, (t * 2 + (c + 1)).value)
                dve.tensor_tensor(on[:, c, :].rearrange("p (h d) -> p h d", d=HD), ps[:, :, 0:HD],
                                  rden[:, c, :].unsqueeze(2).to_broadcast([P, H, HD]), ALU.mult)\
                    .then_inc(drained[b], 1)

            def ev_w(t, p):
                b = BANK["w"]
                dve.wait_ge(filled[b], uses("w", t).value)
                dve.wait_ge(drained[BANK["u"]], uses("u", t).value)
                for c in range(C):
                    ins = dve.scalar_tensor_tensor(out=yT[:, c, :], in0=gen3[b][:, c, :],
                                                   scalar=dcoef[WW][:, c, bass.ds(t.value, 1)], in1=skipT[:, c, :],
                                                   op0=ALU.mult, op1=ALU.add)
                ins.then_inc(drained[b], 1)

            def choose(t, p):
                b = BANK["lg"]
                dve.wait_ge(filled[b], uses("lg", t).value)
                dve.tensor_scalar(lg[:, :, :], gen[b][:, 0:C * NE].rearrange("p (c e) -> p c e", c=C), CLAMP, -CLAMP,
                                  ALU.min, ALU.max).then_inc(drained[b], 1)
                met = ahead(dve, uses("lg", t))
                dve.wait_ge(const_ready, 12)
                dve.wait_ge(drained[b], met)
                for c in range(C):
                    ins = dve.max(top8[:, c, :], lg[:, c, :])
                ins.then_inc(top_ready, 1)
                met = ahead(dve, t + 1)
                dve.wait_ge(const_ready, 12)
                dve.wait_ge(top_ready, met)
                for c in range(C):
                    ins = dve.max_index(idx8[:, c, :], top8[:, c, :], lg[:, c, :])
                ins.then_inc(idx_ready, 1)
                dve.wait_ge(ex_ready, t.value)
                dve.tensor_tensor(gap[:, :], top8[:, :, 1], top8[:, :, 0], ALU.subtract).then_inc(gap_ready, 1)
                dve.wait_ge(idx_ready, (t + 1).value)
                dve.tensor_copy(idxf[:, :, :], idx8[:, :, 0:TOPK]).then_inc(idxf_ready, 1)
                dve.wait_ge(idxf_ready, (t + 1).value)
                for k in range(TOPK):
                    dve.tensor_tensor(onehot[:, :, k, :], expert_no[:, :].unsqueeze(1).to_broadcast([P, C, NE]),
                                      idxf[:, :, k:k + 1].to_broadcast([P, C, NE]), ALU.is_equal)\
                        .then_inc(onehot_ready, 1)
                dve.wait_ge(onehot_ready, (t * 2 + 2).value)
                dve.tensor_tensor(chosen[:, :, :], onehot[:, :, 0, :], onehot[:, :, 1, :], ALU.add)\
                    .then_inc(chosen_ready, 1)

            def route(t, p):
                dve.wait_ge(ex_ready, (t + 1).value)
                dve.tensor_scalar(den[:, :], ex[:, :], 1.0, 1e-12, ALU.add, ALU.add).then_inc(den_ready, 1)
                dve.wait_ge(den_ready, (t * 2 + 1).value)
                dve.reciprocal(pr[:, :, 0], den[:, :]).then_inc(den_ready, 1)
                dve.wait_ge(den_ready, (t * 2 + 2).value)
                dve.tensor_tensor(pr[:, :, 1], ex[:, :], pr[:, :, 0], ALU.mult).then_inc(pr_ready, 1)
                b = BANK["rt"]
                dve.wait_ge(filled[b], uses("rt", t).value)
                ps = gen[b]
                for c in range(C):
                    dve.wait_ge(base_step, (t * 3 + (c + 1)).value)
                    dve.tensor_tensor(base[:, c + 1, :], base[:, c, :], ps[:, (C + c) * NE:(C + c + 1) * NE], ALU.add)\
                        .then_inc(base_step, 1)
                dve.tensor_tensor(pos[:, :, :], ps[:, 0:C * NE].rearrange("p (c e) -> p c e", c=C), base[:, 0:C, :],
                                  ALU.add).then_inc(drained[b], 1)
                dve.wait_ge(drained[b], uses("rt", t).value)
                dve.wait_ge(base_step, (t * 3 + 3).value)
                dve.tensor_copy(base[:, 0, :], base[:, C, :]).then_inc(base_step, 1)
                dve.tensor_scalar(over[:, :, :], pos[:, :, :], float(CAP), FAR, ALU.is_ge, ALU.mult)\
                    .then_inc(over_ready, 1)
                dve.tensor_tensor(place[:, :, :], pos[:, :, :], expert_base[:, :].unsqueeze(1).to_broadcast([P, C, NE]),
                                  ALU.add).then_inc(place_step, 1)
                dve.wait_ge(over_ready, (t + 1).value)
                dve.wait_ge(place_step, (t * 2 + 1).value)
                dve.tensor_tensor(place[:, :, :], place[:, :, :], over[:, :, :], ALU.add).then_inc(place_step, 1)
                dve.wait_ge(place_step, (t * 2 + 2).value)
                for k in range(TOPK):
                    ins = dve.tensor_tensor(picked[:, :, k, :], onehot[:, :, k, :], place[:, :, :], ALU.mult)
                ins.then_inc(picked_ready, 1)
                dve.wait_ge(picked_ready, (t + 1).value)
                dve.tensor_reduce(slot_f[:, :, :], picked[:, :, :, :], AX.X, ALU.add).then_inc(slotf_ready, 1)
                dve.wait_ge(slotf_ready, (t + 1).value)
                dve.wait_ge(entries_out, (t * (C * TOPK * 16)).value)
                dve.tensor_copy(slot_i[:, :, :], slot_f[:, :, :])
                dve.tensor_copy(entry[:, :, :, 0], token_f[:, :].unsqueeze(2).to_broadcast([P, C, TOPK]))\
                    .then_inc(token_read, 1)
                dve.wait_ge(pr_ready, (t + 1).value)
                dve.tensor_copy(entry[:, :, :, 1].bitcast(F32), pr[:, :, :]).then_inc(entry_ready, 1)
                dve.wait_ge(token_read, (t * 2 + 1).value)
                dve.tensor_scalar(token_f[:, :], token_f[:, :], float(S), None, ALU.add).then_inc(token_read, 1)
                dve.wait_ge(token_read, (t * 2 + 2).value)

            def pro():
                for t, p in ((Count(0), 0), (Count(1), 1)):
                    norm(t, p)
                    rest(t, p, "q", WQ, qparts, qrest, q1_ready, q3_ready)
                    rest(t, p, "k", WK, kparts, krest, k1_ready, k3_ready)
                    ev_v(t, p)
                for g in range(4):
                    maxima(Count(0), 0, g)
                minus_max(Count(0), 0)

            def slot(s, p, more):
                if more:
                    norm(s + 2, p)
                if more or p == 0:
                    for g in range(4):
                        maxima(s + 1, 1 - p, g)
                    minus_max(s + 1, 1 - p)
                normalise(s, p, 0)
                normalise(s, p, 1)
                if more:
                    rest(s + 2, p, "q", WQ, qparts, qrest, q1_ready, q3_ready)
                ev_w(s, p)
                if more:
                    rest(s + 2, p, "k", WK, kparts, krest, k1_ready, k3_ready)
                choose(s, p)
                if more:
                    ev_v(s + 2, p)
                route(s, p)

            def take(nb, first):
                dve.wait_ge(up_filled, (nb * FC).value)
                for c in range(C):
                    dve.wait_ge(xeT_filled, (nb * C + (c + 1)).value)
                    dve.tensor_copy(xeT[:, c, :], gen[c][:, :]).then_inc(xeT_ready, 1)

            def blocks(i, more):
                for j in range(2 * NBLK):
                    nb = at(i, j)
                    for f in range(FC):
                        dve.wait_ge(sg_ready, (nb * FC + (f + 1)).value)
                        dve.tensor_tensor(hid[:, f, :], sg[f % 2][:, :], banks[4 + f % 2][:, :], ALU.mult)\
                            .then_inc(h_ready, 1)
                    if more or j < 2 * NBLK - 1:
                        take(nb + 1, False)
                    dve.wait_ge(down_filled, (nb * 2 + 1).value)
                    if last_one(i, j):
                        dve.wait_ge(adds_out, (nb * (JT * 16)).value)
                    for tt in (0, 1):
                        ins = dve.tensor_scalar(ye[:, tt, :], o_ps[0][:, tt * D:(tt + 1) * D],
                                                tab[j % 2][:, tt, 1:2].bitcast(F32), None, ALU.mult)
                    ins.then_inc(ye_dve, 1)

            def last():
                take(Count(0), True)
                with dve.Fori(0, NE // 2 - 1) as i:
                    blocks(i, True)
                blocks(NE // 2 - 1, False)

            slots_of(dve, pro, slot, last)

        @block.tensor
        def _(pe):
            pe.wait_ge(const_ready, 12)
            pe.wait_ge(small_in, 32)
            for c in range(4):
                ins = pe.transpose(banks[2][:, c * B:(c + 1) * B], cond_sb[:, c * P:(c + 1) * P], ident[0:B, 0:B])
            ins.then_inc(set_filled, 1)
            pe.wait_ge(w_in, 5 * 16)
            for n in range(5):
                pe.wait_ge(set_drained, n)
                for ic in range(C):
                    for oc in range(C):
                        ins = pe.transpose(banks[2 + (n + 1) % 2][:, ic * D + oc * P:ic * D + (oc + 1) * P],
                                           wload[n][:, oc, ic * P:(ic + 1) * P], ident[:, :])
                ins.then_inc(set_filled, 1)
            for n in range(5):
                pe.wait_ge(set_drained, n + 5)
                pe.wait_ge(sq_ready, n + 2)
                side = 0 if n < 3 else C
                for oc in range(C):
                    for ic in range(C):
                        ins = pe.matmul(banks[2 + n % 2][:, oc * B:(oc + 1) * B], squares[n][:, ic, oc * P:(oc + 1) * P],
                                        condsq[:, side + ic, :], start=(ic == 0), stop=(ic == C - 1))
                ins.then_inc(set_filled, 1)

            def begin(use, t):
                b = BANK[use]
                pe.wait_ge(drained[b], (uses(use, t) - 1).value)
                return b

            def transposes(dst, src):
                for a in range(C):
                    for c in range(C):
                        ins = pe.transpose(dst[:, a, c * P:(c + 1) * P], src[:, c, a * P:(a + 1) * P], ident[:, :])
                return ins

            def project(b, w, src):
                for m in range(C):
                    for k in range(C):
                        ins = pe.matmul(gen3[b][:, m, :], w[:, k, m * P:(m + 1) * P], src[:, k, :],
                                        start=(k == 0), stop=(k == C - 1))
                ins.then_inc(filled[b], 1)

            def a_xT(t, p):
                b = begin("xT", t)
                pe.wait_ge(xn_ready, (t + 1).value)
                transposes(gen3[b], xn).then_inc(filled[b], 1)

            def a_proj(t, p, use, n):
                pe.wait_ge(drained[BANK["xT"]], uses("xT", t).value)
                project(begin(use, t), wT[n], xT)

            def a_v(t, p):
                b = begin("v", t)
                pe.wait_ge(drained[BANK["vT"]], uses("vT", t).value)
                transposes(gen3[b], vT[p]).then_inc(filled[b], 1)

            def scores(t, p, g):
                if g == 0:
                    pe.wait_ge(stack_in[p], (t * 96 + (192 - 96 * p)).value)
                for h in range(4 * g, 4 * g + 4):
                    pe.wait_ge(s_drained, (t * H + (h - 1)).value)
                    for c in range(C):
                        ins = pe.matmul(sc_ps[h % 2][:, c * S:(c + 1) * S], qst[p][0:KS, h, c * P:(c + 1) * P],
                                        kst[p][0:KS, h, :], start=True, stop=True)
                    ins.then_inc(s_filled, 1)

            def max_t(t, p):
                b = begin("maxT", t)
                pe.wait_ge(s_drained, (t * H + H).value)
                for c in range(C):
                    ins = pe.transpose(gen[b][0:H, c * P:(c + 1) * P], mx[:, c, :], ident[:, :])
                ins.then_inc(filled[b], 1)

            def shifted(t, p, g):
                if g == 0:
                    pe.wait_ge(nm_in, (t * 48 + 48).value)
                for h in range(4 * g, 4 * g + 4):
                    pe.wait_ge(p_ready, (t * H + (h - 1 if h >= 2 else 0)).value)
                    for c in range(C):
                        ins = pe.matmul(st_ps[h % 2][:, c * S:(c + 1) * S], kst[p][0:KM, h, c * P:(c + 1) * P],
                                        qst[p][0:KM, h, :], start=True, stop=True)
                    ins.then_inc(t_filled, 1)

            def values(t, p, g):
                if g == 0:
                    pe.wait_ge(o_drained, (t * 2).value)
                pe.wait_ge(p_ready, (t * H + (4 * g + 4)).value)
                for c in range(C):
                    for j in range(4):
                        h = 4 * g + j
                        ins = pe.matmul(o_ps[g // 2][VW * j:VW * (j + 1), (g % 2) * S:(g % 2 + 1) * S],
                                        vaug[p][:, c, h, :], probs[h % 8][:, c, :], start=(c == 0), stop=(c == C - 1),
                                        skip_group_check=True)
                ins.then_inc(av_done, 1)

            def d_o2(t, p, c):
                use = ("o2a", "o2b")[c]
                b = begin(use, t)
                pe.wait_ge(o_drained, (t * 2 + 2).value)
                for g in range(4):
                    ins = pe.transpose(gen[b][:, g * P:(g + 1) * P], oTa[:, g, c * P:(c + 1) * P], ident[:, :])
                ins.then_inc(filled[b], 1)

            def d_oT(t, p):
                b = begin("oT", t)
                pe.wait_ge(drained[BANK["o2a"]], uses("o2a", t).value)
                pe.wait_ge(drained[BANK["o2b"]], uses("o2b", t).value)
                transposes(gen3[b], on).then_inc(filled[b], 1)

            def d_w(t, p):
                b = begin("w", t)
                pe.wait_ge(drained[BANK["oT"]], uses("oT", t).value)
                project(b, wT[WW], oT)

            def d_u(t, p):
                project(begin("u", t), wT[WU], vT[p])

            def d_y(t, p):
                b = begin("y", t)
                pe.wait_ge(drained[BANK["w"]], uses("w", t).value)
                transposes(gen3[b], yT).then_inc(filled[b], 1)

            def d_lg(t, p):
                b = begin("lg", t)
                for c in range(C):
                    for k in range(C):
                        ins = pe.matmul(gen[b][:, c * NE:(c + 1) * NE], yT[:, k, c * P:(c + 1) * P], wr_sb[:, k, :],
                                        start=(k == 0), stop=(k == C - 1))
                ins.then_inc(filled[b], 1)

            def r_counts(t, p):
                b = begin("rt", t)
                pe.wait_ge(chosen_ready, (t + 1).value)
                pe.matmul(gen[b][:, 0:C * NE], before[:, :], chosen[:, :, :].rearrange("p c e -> p (c e)"),
                          start=True, stop=True)
                pe.matmul(gen[b][:, C * NE:2 * C * NE], ones[:, :], chosen[:, :, :].rearrange("p c e -> p (c e)"),
                          start=True, stop=True).then_inc(filled[b], 1)

            def pro():
                pe.wait_ge(d_ready, 3)
                for t, p in ((Count(0), 0), (Count(1), 1)):
                    a_xT(t, p)
                    a_proj(t, p, "q", WQ)
                    a_proj(t, p, "k", WK)
                    a_proj(t, p, "vT", WV)
                    a_v(t, p)
                for g in range(4):
                    scores(Count(0), 0, g)
                max_t(Count(0), 0)

            def slot(s, p, more):
                for g in range(5):
                    if g < 4:
                        shifted(s, p, g)
                    if g >= 1:
                        if more or p == 0:
                            scores(s + 1, 1 - p, g - 1)
                        values(s, p, g - 1)
                if more or p == 0:
                    max_t(s + 1, 1 - p)
                d_o2(s, p, 0)
                d_o2(s, p, 1)
                if more:
                    a_xT(s + 2, p)
                d_oT(s, p)
                if more:
                    a_proj(s + 2, p, "q", WQ)
                d_w(s, p)
                d_u(s, p)
                if more:
                    a_proj(s + 2, p, "k", WK)
                d_y(s, p)
                d_lg(s, p)
                if more:
                    a_proj(s + 2, p, "vT", WV)
                    a_v(s + 2, p)
                r_counts(s, p)

            def turn(nb, half, b):
                pe.wait_ge(xeT_ready, (nb * C).value)
                pe.wait_ge(xe_in[b], ((half + 1) * (JT * 16)).value)
                for c in range(C):
                    for j in range(JT):
                        ins = pe.transpose(gen[c][:, j * P:(j + 1) * P], xe[b][:, j, c * P:(c + 1) * P], ident[:, :])
                    ins.then_inc(xeT_filled, 1)

            def up(nb, e):
                pe.wait_ge(xeT_ready, (nb * C + C).value)
                for f in range(FC):
                    if f >= 2:
                        pe.wait_ge(h_ready, (nb * FC + (f - 1)).value)
                    for w, bank in ((w1_sb, banks[2 + f % 2]), (w3_sb, banks[4 + f % 2])):
                        for c in range(C):
                            ins = pe.matmul(bank[:, :], w[e][:, c, f * P:(f + 1) * P], xeT[:, c, :],
                                            start=(c == 0), stop=(c == C - 1))
                    ins.then_inc(up_filled, 1)

            def down(nb, e):
                pe.wait_ge(h_ready, (nb * FC + FC).value)
                for tt in range(JT):
                    for f in range(FC):
                        ins = pe.matmul(o_ps[tt // 2][:, (tt % 2) * D:(tt % 2 + 1) * D], hid[:, f, tt * P:(tt + 1) * P],
                                        w2_sb[e][:, f, :], start=(f == 0), stop=(f == FC - 1))
                    if tt % 2:
                        ins.then_inc(down_filled, 1)

            def blocks(i, more):
                for j in range(2 * NBLK):
                    nb = at(i, j)
                    if j % NBLK == 0:
                        pe.wait_ge(wexp_in[j // NBLK], (Count(i * 48 + 48) if isinstance(i, int) else Count(48, 48, i)).value)
                    up(nb, j // NBLK)
                    half = Count(i * NBLK + (j + 1) // 2) if isinstance(i, int) else Count((j + 1) // 2, NBLK, i)
                    if more or j < 2 * NBLK - 1:
                        turn(nb + 1, half, (j + 1) % 2)
                    down(nb, j // NBLK)

            def last():
                for b in (0, 1):
                    pe.wait_ge(drained[b], BANK_TOTAL[b])
                turn(Count(0), Count(0), 0)
                with pe.Fori(0, NE // 2 - 1) as i:
                    blocks(i, True)
                blocks(NE // 2 - 1, False)

            slots_of(pe, pro, slot, last)


_INS = ["x", "cond_2048", "L0_cond_q_weight", "L0_cond_k_weight", "L0_cond_v_weight", "L0_cond_w_weight",
        "L0_cond_u_weight", "L0_ffn_Wr", "L0_ffn_W1", "L0_ffn_W3", "L0_ffn_W2"]


def kernel(**inputs):
    import numpy as _np
    import concourse.bacc as _bacc
    from concourse import mybir as _mybir
    from concourse.bass_utils import run_bass_kernel_spmd as _run

    nc = _bacc.Bacc("TRN2", target_bir_lowering=False, num_devices=1)
    arrays, args = {}, []
    for name in _INS:
        a = _np.ascontiguousarray(inputs[name])
        arrays[f"in_{name}"] = a
        args.append(nc.dram_tensor(f"in_{name}", a.shape, _mybir.dt.from_np(a.dtype), kind="ExternalInput").ap())
    out = nc.dram_tensor("out_x", (B, S, D), _mybir.dt.from_np(_np.dtype("float32")), kind="ExternalOutput").ap()
    adaln_moe(nc, *args, out)
    r = _run(nc, [arrays], core_ids=[0])
    return r.results[0]["out_x"]
```

```python
from contextlib import ExitStack

import concourse.bass as bass
from concourse import mybir

ALU = mybir.AluOpType
ACT = mybir.ActivationFunctionType
AX = mybir.AxisListType
F32 = mybir.dt.float32
F32R = mybir.dt.float32r
BF16 = mybir.dt.bfloat16
I32 = mybir.dt.int32
U32 = mybir.dt.uint32

P = 128
B, S, D = 32, 256, 256
H, HD = 16, 16
NE, F, TOPK = 8, 1024, 2
T = B * S
CAP = -(-T * TOPK * 5 // (4 * NE))
C = D // P
FC = F // P
BLK = 512
JT = BLK // P
NBLK = CAP // BLK
PIECES = 6
PIECE = 3 * C * F // PIECES
assert NBLK * BLK == CAP and S == D == C * P
CONSTANTS = 14
CLAMP = 10000.0
FAR = 65536.0
Q_RUNS = ((0, 3, 0, False), (3, 2, 0, False), (5, 1, 0, False))
K_RUNS = ((0, 3, 0, True), (3, 2, 1, True), (5, 1, 2, True))
KS = HD * 6
KM = KS + 3
STACK_LOADS = sum(pairs if same else 1 for _, pairs, _, same in Q_RUNS + K_RUNS)
HG = H // C
LAG = 4
VW = 32

BANK = {"xT": 0, "o2a": 1, "o2b": 0, "q": 1, "k": 0, "oT": 1, "w": 0, "lg": 1, "y": 0, "u": 1,
        "vT": 0, "rt": 1, "v": 0, "maxT": 1}
SLOT_USES = (("xT", 2), ("o2a", -1), ("o2b", -1), ("q", 2), ("k", 2), ("oT", -1), ("w", -1), ("lg", -1),
             ("y", -1), ("u", 0), ("vT", 2), ("rt", -1), ("v", 1), ("maxT", 1))
PRO_USES = (("xT", 0), ("q", 0), ("k", 0), ("vT", 0), ("v", 0), ("xT", 1), ("q", 1), ("k", 1), ("vT", 1), ("maxT", 0))


def bank_counts():
    n, at = [0, 0], {}

    def use(name, t):
        n[BANK[name]] += 1
        at[name, t] = n[BANK[name]]

    for name, t in PRO_USES:
        use(name, t)
    for s in range(B + 1):
        for name, ahead_by in SLOT_USES:
            if 0 <= s + ahead_by < B:
                use(name, s + ahead_by)
    return at, n


COUNTS, BANK_TOTAL = bank_counts()


class Count:

    def __init__(self, first, step=0, i=None):
        self.first, self.step, self.i = first, step, i

    def __add__(self, n):
        return Count(self.first + n, self.step, self.i)

    def __sub__(self, n):
        return self + -n

    def __mul__(self, n):
        return Count(self.first * n, self.step * n, self.i)

    @property
    def value(self):
        return max(self.first, 0) if self.i is None else self.i * self.step + self.first


def uses(name, t):
    if t.i is None:
        return Count(COUNTS[name, t.first])
    at = [COUNTS[name, t.first + n * t.step] for n in (1, 2, 3)]
    assert at[2] - at[1] == at[1] - at[0]
    return Count(2 * at[0] - at[1], at[1] - at[0], t.i)


def ahead(eng, count):
    return count.value if count.i is None else eng.compute_val(count.value)


def adaln_moe(nc, x, cond, wq, wk, wv, ww, wu, wr, w1, w3, w2, out):
    with ExitStack() as ctx:
        phase = ctx.enter_context(ExitStack())

        def sb(name, shape, dt=F32):
            return ctx.enter_context(nc.sbuf_tensor(name, shape, dt))

        def sb_attention(name, shape, dt=F32):
            return phase.enter_context(nc.sbuf_tensor(name, shape, dt))

        def pb(name):
            return ctx.enter_context(nc.psum_tensor(name, [P, 512], F32))

        def sem(name):
            return ctx.enter_context(nc.semaphore(name))

        y_rows = nc.dram_tensor("y_rows", [T, D], F32, kind="Internal").ap()
        slots = nc.dram_tensor("slot_table", [NE * CAP, 2], I32, kind="Internal").ap()
        parts_rows = nc.dram_tensor("parts_rows", [2, 2, C, 3, P, S], BF16, kind="Internal").ap()
        x_rows = x.rearrange("b s d -> (b s) d")
        out_rows = out.rearrange("b s d -> (b s) d")

        ident = sb("ident", [P, P])
        before = sb("before", [P, P], BF16)
        ones = sb("ones", [P, P], BF16)
        expert_no = sb("expert_no", [P, NE])
        expert_no_i = sb("expert_no_i", [P, NE], I32)
        expert_base = sb("expert_base", [P, NE])
        token_no = sb("token_no", [P, C], I32)
        token_f = sb("token_f", [P, C])
        empty = sb("empty", [P, NE * CAP // P, 2], I32)
        w_raw = sb("w_raw", [P, 3, C * F])
        w_hi0 = sb("w_hi0", [P, 3, C * F], F32R)
        w_lo0 = sb("w_lo0", [P, 3, C * F], F32R)
        tab = [sb(f"tab{p}", [P, JT, 2], I32) for p in (0, 1)]
        xe = [sb(f"xe{p}", [P, JT, D]) for p in (0, 1)]
        wT = [sb_attention(f"wT{n}", [P, C, D]) for n in range(5)]
        wr_sb = sb_attention("wr_sb", [P, C, NE])
        cond_sb = sb_attention("cond_sb", [B, 2 * D])
        condT = sb_attention("condT", [P, 4, B])
        condsq = sb_attention("condsq", [P, 4, B])
        dcoef = [sb_attention(f"dcoef{n}", [P, C, B]) for n in range(5)]
        x_tok = [sb_attention(f"x_tok{p}", [P, C, D]) for p in (0, 1)]
        s1_all = [sb_attention(f"s1_all{p}", [P, D]) for p in (0, 1)]
        xs = sb_attention("xs", [P, C, D])
        stats = sb_attention("stats", [P, C, 6])
        mv = sb_attention("mv", [P, C, 2])
        var = sb_attention("var", [P, C])
        rstd = sb_attention("rstd", [P, C])
        minus_half = sb_attention("minus_half", [P, C * B])
        xn = sb_attention("xn", [P, C, D])
        xT = sb_attention("xT", [P, C, S])
        qparts = sb_attention("qparts", [P, C, 3, S], BF16)
        kparts = sb_attention("kparts", [P, C, 3, S], BF16)
        qrest = sb_attention("qrest", [P, C, S])
        krest = sb_attention("krest", [P, C, S])
        vT = [sb_attention(f"vT{p}", [P, C, S]) for p in (0, 1)]
        vaug = [sb_attention(f"vaug{p}", [P, C, H, VW]) for p in (0, 1)]
        qst = [sb_attention(f"qst{p}", [P, H, S], BF16) for p in (0, 1)]
        kst = [sb_attention(f"kst{p}", [P, H, S], BF16) for p in (0, 1)]
        mx = sb_attention("mx", [P, C, H])
        nm = sb_attention("nm", [H, 3, S], BF16)
        nrest = sb_attention("nrest", [H, S])
        probs = [sb_attention(f"probs{n}", [P, C, S]) for n in range(8)]
        wload = probs
        oTa = sb_attention("oTa", [P, 4, S])
        rden = sb_attention("rden", [P, C, H])
        on = sb_attention("on", [P, C, D])
        oT = sb_attention("oT", [P, C, S])
        skipT = sb_attention("skipT", [P, C, S])
        yT = sb_attention("yT", [P, C, S])
        y_tok = sb_attention("y_tok", [P, C, D])
        lg = sb_attention("lg", [P, C, NE])
        top8 = sb_attention("top8", [P, C, 8])
        idx8 = sb_attention("idx8", [P, C, 8], U32)
        idxf = sb_attention("idxf", [P, C, TOPK])
        onehot = sb_attention("onehot", [P, C, TOPK, NE])
        chosen = sb_attention("chosen", [P, C, NE], BF16)
        gap = sb_attention("gap", [P, C])
        ex = sb_attention("ex", [P, C])
        den = sb_attention("den", [P, C])
        pr = sb_attention("pr", [P, C, TOPK])
        base = sb_attention("base", [P, C + 1, NE])
        pos = sb_attention("pos", [P, C, NE])
        over = sb_attention("over", [P, C, NE])
        place = sb_attention("place", [P, C, NE])
        picked = sb_attention("picked", [P, C, TOPK, NE])
        slot_f = sb_attention("slot_f", [P, C, TOPK])
        slot_i = sb_attention("slot_i", [P, C, TOPK], U32)
        entry = sb_attention("entry", [P, C, TOPK, 2], I32)
        squares = [probs[5], probs[6], probs[7], xn, on]
        phase.close()

        w_hi = [w_hi0, sb("w_hi1", [P, 3, C * F], F32R)]
        w_lo = [w_lo0, sb("w_lo1", [P, 3, C * F], F32R)]
        xeT_hi = sb("xeT_hi", [P, C, BLK], F32R)
        xeT_lo = sb("xeT_lo", [P, C, BLK], F32R)
        sg = [sb(f"sg{p}", [P, BLK]) for p in (0, 1)]
        hid = [sb(f"hid{p}", [P, BLK]) for p in (0, 1)]
        hid_hi = sb("hid_hi", [P, FC, BLK], F32R)
        hid_lo = sb("hid_lo", [P, FC, BLK], F32R)
        ye = sb("ye", [P, JT, D])

        banks = [pb(f"bank{n}") for n in range(8)]
        gen = banks[0:2]
        sc_ps = banks[2:4]
        st_ps = banks[4:6]
        o_ps = banks[6:8]
        gen3 = [g[:, :].rearrange("p (c n) -> p c n", c=C) for g in gen]

        filled = [sem(f"bank{n}_filled") for n in (0, 1)]
        drained = [sem(f"bank{n}_drained") for n in (0, 1)]
        w_in = sem("w_in")
        small_in = sem("small_in")
        const_ready = sem("const_ready")
        const_step = sem("const_step")
        rows_zero = sem("rows_zero")
        set_filled = sem("set_filled")
        set_drained = sem("set_drained")
        sq_ready = sem("sq_ready")
        numbers_ready = sem("numbers_ready")
        roots_ready = sem("roots_ready")
        d_ready = sem("d_ready")
        table_empty = sem("table_empty")
        out_is_x = sem("out_is_x")
        x_in = [sem(f"x_in{p}") for p in (0, 1)]
        xs_ready = sem("xs_ready")
        stats_ready = sem("stats_ready")
        aggr_ready = sem("aggr_ready")
        var_ready = sem("var_ready")
        rstd_ready = sem("rstd_ready")
        xn_ready = sem("xn_ready")
        q1_ready = sem("q1_ready")
        k1_ready = sem("k1_ready")
        q2_ready = sem("q2_ready")
        k2_ready = sem("k2_ready")
        q3_ready = sem("q3_ready")
        k3_ready = sem("k3_ready")
        parts_out = [sem(f"{n}_parts_out") for n in "qk"]
        stack_in = [[sem(f"stack{half}_in{p}") for p in (0, 1)] for half in range(C)]
        s_filled = sem("s_filled")
        s_drained = sem("s_drained")
        n1_ready = sem("n1_ready")
        n2_ready = sem("n2_ready")
        n3_ready = sem("n3_ready")
        nm_in = sem("nm_in")
        t_filled = sem("t_filled")
        p_ready = sem("p_ready")
        av_done = sem("av_done")
        o_drained = sem("o_drained")
        rden_ready = sem("rden_ready")
        y_out = sem("y_out")
        top_ready = sem("top_ready")
        idx_ready = sem("idx_ready")
        idxf_ready = sem("idxf_ready")
        onehot_ready = sem("onehot_ready")
        chosen_ready = sem("chosen_ready")
        gap_ready = sem("gap_ready")
        ex_ready = sem("ex_ready")
        den_ready = sem("den_ready")
        pr_ready = sem("pr_ready")
        base_step = sem("base_step")
        pos_ready = sem("pos_ready")
        over_ready = sem("over_ready")
        place_step = sem("place_step")
        picked_ready = sem("picked_ready")
        slotf_ready = sem("slotf_ready")
        token_read = sem("token_read")
        entry_ready = sem("entry_ready")
        entries_out = sem("entries_out")
        w_raw_in = sem("w_raw_in")
        w_hi_ready = sem("w_hi_ready")
        w_lo_ready = sem("w_lo_ready")
        tab_in = sem("tab_in")
        xe_zero = sem("xe_zero")
        xe_in = [sem(f"xe_in{p}") for p in (0, 1)]
        xeT_filled = sem("xeT_filled")
        xeT_hi_ready = sem("xeT_hi_ready")
        xeT_lo_ready = sem("xeT_lo_ready")
        up_filled = sem("up_filled")
        sg_ready = sem("sg_ready")
        h_ready = sem("h_ready")
        h_hi_ready = sem("h_hi_ready")
        h_lo_ready = sem("h_lo_ready")
        down_filled = sem("down_filled")
        ye_act = sem("ye_act")
        ye_dve = sem("ye_dve")
        adds_out = sem("adds_out")

        weights = (wq, wk, wv, ww, wu)
        WQ, WK, WV, WW, WU = range(5)

        block = ctx.enter_context(nc.Block())

        def at(i, j):
            return Count(i * 2 * NBLK + j) if isinstance(i, int) else Count(j, 2 * NBLK, i)

        def piece(w, n):
            return w[:, n // 2, (n % 2) * PIECE:(n % 2 + 1) * PIECE]

        def pieces_at(i, j):
            if j % NBLK not in (1, 2, 3) or (isinstance(i, int) and j >= NBLK):
                return None, ()
            p, n = j // NBLK, 2 * (j % NBLK - 1)
            return (Count(2 * i + p + 1) if isinstance(i, int) else Count(p + 1, 2, i)), (n, n + 1)

        def last_one(i, j):
            return isinstance(i, int) and j == 2 * NBLK - 1

        def has(s, ahead_by):
            return s.i is not None or 0 <= s.first + ahead_by < B

        def slots_of(eng, pro, slot, last):
            pro()
            for s in (0, 1, 2):
                slot(Count(s), s % 2)
            with eng.Fori(1, (B - 4) // 2) as i:
                slot(Count(1, 2, i), 1)
                slot(Count(2, 2, i), 0)
            for s in range(B - 3, B + 1):
                slot(Count(s), s % 2)
            last()

        @block.sync
        def _(sp):
            for n, w in enumerate(weights):
                sp.dma_start(wload[n][:, :, :], w.rearrange("(c p) i -> p c i", p=P)).then_inc(w_in, 16)
            sp.dma_start(cond_sb[:, :], cond).then_inc(small_in, 16)
            sp.dma_start(wr_sb[:, :, :], wr.rearrange("(c p) e -> p c e", p=P)).then_inc(small_in, 16)

            def load_x(t, p):
                met = ahead(sp, t - 1)
                sp.wait_ge(const_ready, CONSTANTS)
                sp.wait_ge(xs_ready, met)
                sp.dma_start(x_tok[p][:, :, :], x[bass.ds(t.value, 1), :, :].rearrange("b (c p) d -> p (b c) d", p=P))\
                    .then_inc(x_in[p], 16)
                sp.dma_start(s1_all[p][:, :], cond[bass.ds(t.value, 1), 0:D].to_broadcast([P, D])).then_inc(x_in[p], 16)

            def store_parts(t, p):
                for n, (parts, first, third) in enumerate(((qparts, q1_ready, q3_ready), (kparts, k1_ready, k3_ready))):
                    sp.wait_ge(first, (t + 1).value)
                    sp.wait_ge(third, (t + 1).value)
                    sp.dma_start(parts_rows[n, p].rearrange("c n m s -> m c n s"), parts[:, :, :, :])\
                        .then_inc(parts_out[n], 16)

            def load_stack(t, p, half):
                met = ahead(sp, t * 16 + 16)
                sp.wait_ge(const_ready, CONSTANTS)
                sp.wait_ge(parts_out[0], met)
                sp.wait_ge(parts_out[1], (t * 16 + 16).value)
                sp.wait_ge(t_filled, ((t - 2) * H + HG * (half + 1)).value)
                for n, st, runs in ((0, qst, Q_RUNS), (1, kst, K_RUNS)):
                    for row, pairs, part, same in runs:
                        src = parts_rows[n, p, half, part:part + (1 if same else pairs)]\
                            .rearrange("n (d h) s -> (n d) (h s)", h=HG)
                        for r in range(pairs if same else 1):
                            rows = slice((row + r) * HD, (row + (r + 1 if same else pairs)) * HD)
                            sp.dma_start(st[p][rows, half * HG:(half + 1) * HG, :].rearrange("r h s -> r (h s)"), src)\
                                .then_inc(stack_in[half][p], 16)

            def max_rows(t, p):
                met = ahead(sp, t + 1)
                sp.wait_ge(const_ready, CONSTANTS)
                sp.wait_ge(n3_ready, met)
                sp.wait_ge(t_filled, ((t - 1) * H).value)
                for n in range(3):
                    sp.dma_start(qst[p][KS + n:KS + n + 1, :, :], nm[:, n, :]).then_inc(nm_in, 16)

            def store_y(t, p):
                met = ahead(sp, uses("y", t))
                sp.wait_ge(const_ready, CONSTANTS)
                sp.wait_ge(drained[BANK["y"]], met)
                sp.dma_start(y_rows[bass.ds((t * S).value, S), :].rearrange("(c p) d -> p c d", p=P), y_tok[:, :, :])\
                    .then_inc(y_out, 16)

            def load_expert(e):
                for n, src in enumerate((w1, w3)):
                    sp.dma_start(w_raw[:, n, :].rearrange("p (c f) -> p c f", c=C),
                                 src[bass.ds(e.value, 1), :, :].rearrange("e (c p) f -> p (e c) f", p=P))\
                        .then_inc(w_raw_in, 16)
                sp.dma_start(w_raw[:, 2, :].rearrange("p (c d) -> p c d", c=FC),
                             w2[bass.ds(e.value, 1), :, :].rearrange("e (c p) d -> p (e c) d", p=P))\
                    .then_inc(w_raw_in, 16)

            def pro():
                load_x(Count(0), 0)
                load_x(Count(1), 1)
                store_parts(Count(0), 0)
                load_stack(Count(0), 0, 0)
                load_stack(Count(0), 0, 1)
                load_x(Count(2), 0)
                store_parts(Count(1), 1)
                load_stack(Count(1), 1, 0)
                max_rows(Count(0), 0)
                load_stack(Count(1), 1, 1)
                sp.dma_start(out_rows.rearrange("(p n) d -> p (n d)", p=P),
                             x_rows.rearrange("(p n) d -> p (n d)", p=P)).then_inc(out_is_x, 16)
                load_expert(Count(0))

            def slot(s, p):
                if has(s, 3):
                    load_x(s + 3, 1 - p)
                if has(s, 2):
                    store_parts(s + 2, p)
                if has(s, -1):
                    store_y(s - 1, 1 - p)
                if has(s, 2):
                    load_stack(s + 2, p, 0)
                if has(s, 1):
                    max_rows(s + 1, 1 - p)
                if has(s, 2):
                    load_stack(s + 2, p, 1)

            def last():
                with sp.Fori(1, NE) as i:
                    e = Count(0, 1, i)
                    met = ahead(sp, e * PIECES)
                    sp.wait_ge(const_ready, CONSTANTS)
                    sp.wait_ge(w_lo_ready, met)
                    load_expert(e)

            slots_of(sp, pro, slot, last)
            sp.wait_ge(adds_out, NE * NBLK * JT * 16)
            sp.wait_ge(y_out, B * 16)

        @block.gpsimd
        def _(pool):
            pool.memset(ident[:, :], 0.0).then_inc(const_step, 1)
            pool.memset(before[:, :], 1.0).then_inc(const_step, 1)
            pool.wait_ge(const_step, 2)
            pool.affine_select(out=ident[:, :], in_=ident[:, :], compare_op=ALU.not_equal, fill=1.0, base=0,
                               pattern=[[-1, P]], channel_multiplier=1).then_inc(const_ready, 1)
            pool.affine_select(out=before[:, :], in_=before[:, :], compare_op=ALU.is_gt, fill=0.0, base=0,
                               pattern=[[1, P]], channel_multiplier=-1).then_inc(const_ready, 1)
            pool.memset(ones[:, :], 1.0).then_inc(const_ready, 1)
            pool.memset(minus_half[:, :], -0.5).then_inc(const_ready, 1)
            pool.iota(expert_no_i[:, :], pattern=[[1, NE]], base=0, channel_multiplier=0).then_inc(const_ready, 1)
            pool.iota(token_no[:, :], pattern=[[P, C]], base=0, channel_multiplier=1).then_inc(const_ready, 1)
            for p in (0, 1):
                pool.memset(vaug[p][:, :, :, :], 0.0).then_inc(const_step, 1)
                pool.memset(xe[p][:, :, :], 0.0).then_inc(xe_zero, 1)
            pool.memset(empty[:, :, 0], T).then_inc(const_ready, 1)
            pool.memset(empty[:, :, 1], 0).then_inc(const_ready, 1)
            pool.wait_ge(const_step, 4)
            for p in (0, 1):
                pool.memset(vaug[p][:, :, :, HD:HD + 1], 1.0).then_inc(const_ready, 1)
            pool.wait_ge(const_ready, CONSTANTS)
            pool.dma_start(slots.rearrange("(p n) w -> p (n w)", p=P), empty[:, :, :].rearrange("p n w -> p (n w)"))\
                .then_inc(table_empty, 16)

            for n in range(5):
                pool.wait_ge(set_drained, n + 7)
                pool.tensor_tensor(dcoef[n][:, :, :], dcoef[n][:, :, :],
                                   minus_half[:, :].rearrange("p (c b) -> p c b", c=C), ALU.pow)\
                    .then_inc(roots_ready, 1)

            def scale_x(t, p):
                pool.wait_ge(x_in[p], (t * 16 + (32 - 16 * p)).value)
                pool.wait_ge(xn_ready, t.value)
                pool.tensor_tensor(xs[:, :, :], x_tok[p][:, :, :],
                                   s1_all[p][:, :].unsqueeze(1).to_broadcast([P, C, D]), ALU.mult)\
                    .then_inc(xs_ready, 1)

            def inverse_root(t):
                pool.wait_ge(var_ready, (t + 1).value)
                pool.tensor_tensor(rstd[:, :], var[:, :], minus_half[:, 0:C], ALU.pow).then_inc(rstd_ready, 1)

            def small_parts(t, use, parts, rest, second, third):
                met = ahead(pool, uses(use, t))
                pool.wait_ge(const_ready, CONSTANTS)
                pool.wait_ge(drained[BANK[use]], met)
                pool.tensor_copy(parts[:, :, 1, :], rest[:, :, :]).then_inc(second, 1)
                pool.wait_ge(second, (t + 1).value)
                pool.tensor_tensor(parts[:, :, 2, :], rest[:, :, :], parts[:, :, 1, :], ALU.subtract)\
                    .then_inc(third, 1)

            def split(t, p):
                small_parts(t, "q", qparts, qrest, q2_ready, q3_ready)
                small_parts(t, "k", kparts, krest, k2_ready, k3_ready)

            def enter(t, p):
                met = ahead(pool, t + 1)
                pool.wait_ge(const_ready, CONSTANTS)
                pool.wait_ge(entry_ready, met)
                for c in range(C):
                    for k in range(TOPK):
                        pool.indirect_dma_start(
                            out=slots, out_offset=bass.IndirectOffsetOnAxis(ap=slot_i[:, c, k:k + 1], axis=0),
                            in_=entry[:, c, k, :], in_offset=None, bounds_check=NE * CAP - 1, oob_is_err=False)\
                            .then_inc(entries_out, 16)

            def pro():
                for t, p in ((Count(0), 0), (Count(1), 1)):
                    scale_x(t, p)
                    inverse_root(t)
                    split(t, p)
                scale_x(Count(2), 0)
                inverse_root(Count(2))
                pool.wait_ge(table_empty, 16)

            def slot(s, p):
                if has(s, 2):
                    split(s + 2, p)
                if has(s, 3):
                    scale_x(s + 3, 1 - p)
                if has(s, -1):
                    enter(s - 1, 1 - p)
                if has(s, 3):
                    inverse_root(s + 3)

            def fetch(nb, b):
                pool.dma_start(tab[b][:, :, :], slots[bass.ds((nb * BLK).value, BLK), :].rearrange("(p j) w -> p j w", j=JT))\
                    .then_inc(tab_in, 16)
                met = ahead(pool, nb * 16 + 16)
                pool.wait_ge(const_ready, CONSTANTS)
                pool.wait_ge(tab_in, met)
                for j in range(JT):
                    pool.indirect_dma_start(
                        out=xe[b][:, j, :], out_offset=None, in_=y_rows,
                        in_offset=bass.IndirectOffsetOnAxis(ap=tab[b][:, j, 0:1].bitcast(U32), axis=0),
                        bounds_check=T - 1, oob_is_err=False).then_inc(xe_in[b], 16)

            def add(nb, b):
                met = ahead(pool, nb + 1)
                pool.wait_ge(const_ready, CONSTANTS)
                pool.wait_ge(ye_act, met)
                pool.wait_ge(ye_dve, (nb + 1).value)
                for j in range(JT):
                    pool.indirect_dma_start(
                        out=out_rows, out_offset=bass.IndirectOffsetOnAxis(ap=tab[b][:, j, 0:1].bitcast(U32), axis=0),
                        in_=ye[:, j, :], in_offset=None, bounds_check=T - 1, oob_is_err=False,
                        compute_op=ALU.add).then_inc(adds_out, 16)

            def last():
                pool.wait_ge(entries_out, B * C * TOPK * 16)
                pool.wait_ge(y_out, B * 16)
                pool.wait_ge(xe_zero, 2)
                pool.wait_ge(out_is_x, 16)
                fetch(Count(0), 0)

                def blocks(i, more):
                    for j in range(2 * NBLK):
                        if more or j < 2 * NBLK - 1:
                            fetch(at(i, j + 1), (j + 1) % 2)
                        add(at(i, j), j % 2)
                        met = ahead(pool, (at(i, j) + 1) * (JT * 16))
                        pool.wait_ge(const_ready, CONSTANTS)
                        pool.wait_ge(adds_out, met)

                with pool.Fori(0, NE // 2 - 1) as i:
                    blocks(i, True)
                blocks(NE // 2 - 1, False)

            slots_of(pool, pro, slot, last)

        @block.scalar
        def _(act):
            act.wait_ge(d_ready, 3)

            def ev_xT(t, p):
                b = BANK["xT"]
                act.wait_ge(filled[b], uses("xT", t).value)
                act.activation(xT[:, :, :], gen3[b], ACT.Copy).then_inc(drained[b], 1)

            def first_part(t, p, use, n, parts, first):
                b = BANK[use]
                act.wait_ge(filled[b], uses(use, t).value)
                for c in range(C):
                    ins = act.activation(parts[:, c, 0, :], gen3[b][:, c, :], ACT.Copy,
                                         scale=dcoef[n][:, c, bass.ds(t.value, 1)])
                ins.then_inc(first, 1)

            def parts_free(t, n):
                act.wait_ge(parts_out[n], (t * 16).value)

            def ev_vT(t, p):
                b = BANK["vT"]
                act.wait_ge(filled[b], uses("vT", t).value)
                for c in range(C):
                    ins = act.activation(vT[p][:, c, :], gen3[b][:, c, :], ACT.Copy,
                                         scale=dcoef[WV][:, c, bass.ds(t.value, 1)])
                ins.then_inc(drained[b], 1)

            def exps(t, p, h):
                if h in (8, 12):
                    act.wait_ge(av_done, (t * 4 + (h // 4 - 1)).value)
                act.wait_ge(t_filled, (t * H + (h + 1)).value)
                act.activation(probs[h % 8][:, :, :], st_ps[h % 2][:, :].rearrange("p (c q) -> p c q", c=C),
                               ACT.Exp).then_inc(p_ready, 1)

            def ev_o(t, p, n):
                act.wait_ge(av_done, (t * 4 + (2 * n + 2)).value)
                act.activation(oTa[:, 2 * n:2 * n + 2, :], o_ps[n][:, :].rearrange("p (g q) -> p g q", g=2), ACT.Copy)\
                    .then_inc(o_drained, 1)

            def ev_oT(t, p):
                b = BANK["oT"]
                act.wait_ge(filled[b], uses("oT", t).value)
                act.activation(oT[:, :, :], gen3[b], ACT.Copy).then_inc(drained[b], 1)

            def ev_u(t, p):
                b = BANK["u"]
                act.wait_ge(filled[b], uses("u", t).value)
                for c in range(C):
                    ins = act.activation(skipT[:, c, :], gen3[b][:, c, :], ACT.Copy,
                                         scale=dcoef[WU][:, c, bass.ds(t.value, 1)])
                ins.then_inc(drained[b], 1)

            def ev_y(t, p):
                b = BANK["y"]
                act.wait_ge(y_out, (t * 16).value)
                act.wait_ge(filled[b], uses("y", t).value)
                act.activation(y_tok[:, :, :], gen3[b], ACT.Copy).then_inc(drained[b], 1)

            def ex_gap(t, p):
                act.wait_ge(gap_ready, (t + 1).value)
                act.wait_ge(pr_ready, t.value)
                act.activation(ex[:, :], gap[:, :], ACT.Exp).then_inc(ex_ready, 1)

            def pro():
                for t, p in ((Count(0), 0), (Count(1), 1)):
                    ev_xT(t, p)
                    parts_free(t, 0)
                    first_part(t, p, "q", WQ, qparts, q1_ready)
                    parts_free(t, 1)
                    first_part(t, p, "k", WK, kparts, k1_ready)
                    ev_vT(t, p)

            def split_high(e, p, n):
                act.wait_ge(w_raw_in, (e * 48 + 48).value)
                act.activation(piece(w_hi[p], n), piece(w_raw, n), ACT.Copy).then_inc(w_hi_ready, 1)

            def take_high(nb):
                act.wait_ge(up_filled, (nb * FC).value)
                for c in range(C):
                    act.wait_ge(xeT_filled, (nb * C + (c + 1)).value)
                    act.activation(xeT_hi[:, c, :], gen[c][:, :], ACT.Copy).then_inc(xeT_hi_ready, 1)

            def hidden_high(nb, f):
                act.wait_ge(h_ready, (nb * FC + (f + 1)).value)
                act.activation(hid_hi[:, f, :], hid[f % 2][:, :], ACT.Copy).then_inc(h_hi_ready, 1)

            def slot(s, p):
                for i in range(H + LAG):
                    if i >= LAG and has(s, 0):
                        exps(s, p, i - LAG)
                    if i == 0 and has(s, 2):
                        ev_xT(s + 2, p)
                    if i == 2 and has(s, 2):
                        parts_free(s + 2, 0)
                        first_part(s + 2, p, "q", WQ, qparts, q1_ready)
                    if i == 3 and has(s, 2):
                        parts_free(s + 2, 1)
                        first_part(s + 2, p, "k", WK, kparts, k1_ready)
                    if i == 4 and has(s, -1):
                        ev_oT(s - 1, 1 - p)
                    if i == 9 and has(s, -1):
                        ev_y(s - 1, 1 - p)
                    if i == 10 and has(s, 0):
                        ev_u(s, p)
                    if i == 11 and has(s, 2):
                        ev_vT(s + 2, p)
                    if i == 12 and has(s, -1):
                        ex_gap(s - 1, 1 - p)
                    if i == 14 and has(s, 0):
                        ev_o(s, p, 0)
                if has(s, 0):
                    ev_o(s, p, 1)
                for n in range(PIECES):
                    if s.i is None and s.first == B - 2 + n // 2:
                        split_high(Count(0), 0, n)

            def blocks(i, more):
                for j in range(2 * NBLK):
                    nb = at(i, j)
                    for f in range(FC):
                        act.wait_ge(up_filled, (nb * FC + (f + 1)).value)
                        act.activation(sg[f % 2][:, :], banks[2 + f % 2][:, :], ACT.Silu).then_inc(sg_ready, 1)
                        if f >= 1:
                            hidden_high(nb, f - 1)
                    hidden_high(nb, FC - 1)
                    if more or j < 2 * NBLK - 1:
                        take_high(nb + 1)
                    e, these = pieces_at(i, j)
                    for n in these:
                        split_high(e, 1 - j // NBLK, n)
                    act.wait_ge(down_filled, (nb * 2 + 2).value)
                    if last_one(i, j):
                        act.wait_ge(adds_out, (nb * (JT * 16)).value)
                    for tt in (2, 3):
                        ins = act.activation(ye[:, tt, :], o_ps[1][:, (tt - 2) * D:(tt - 1) * D], ACT.Copy,
                                             scale=tab[j % 2][:, tt, 1:2].bitcast(F32))
                    ins.then_inc(ye_act, 1)

            def last():
                take_high(Count(0))
                with act.Fori(0, NE // 2 - 1) as i:
                    blocks(i, True)
                blocks(NE // 2 - 1, False)

            slots_of(act, pro, slot, last)

        @block.vector
        def _(dve):
            for p in (0, 1):
                dve.memset(kst[p][KS:P, :, :], 0.0).then_inc(rows_zero, 1)
                dve.memset(qst[p][KS:P, :, :], 0.0).then_inc(const_ready, 1)
            dve.wait_ge(rows_zero, 2)
            for p in (0, 1):
                dve.memset(kst[p][KS:KM, :, :], 1.0).then_inc(const_ready, 1)
            dve.wait_ge(const_ready, CONSTANTS)
            dve.tensor_copy(expert_no[:, :], expert_no_i[:, :]).then_inc(numbers_ready, 1)
            dve.tensor_copy(token_f[:, :], token_no[:, :]).then_inc(numbers_ready, 1)
            dve.memset(base[:, 0, :], 0.0).then_inc(base_step, 1)
            dve.wait_ge(numbers_ready, 2)
            dve.tensor_scalar(expert_base[:, :], expert_no[:, :], float(CAP), None, ALU.mult).then_inc(d_ready, 1)
            dve.wait_ge(set_filled, 1)
            dve.tensor_copy(condT[:, :, :], banks[2][:, 0:4 * B].rearrange("p (c b) -> p c b", c=4))\
                .then_inc(set_drained, 1)
            dve.wait_ge(set_drained, 1)
            dve.tensor_tensor(condsq[:, :, :], condT[:, :, :], condT[:, :, :], ALU.mult).then_inc(sq_ready, 1)
            for n in range(5):
                dve.wait_ge(set_filled, n + 2)
                src = banks[2 + (n + 1) % 2][:, :].rearrange("p (c o) -> p c o", c=C)
                for c in range(C):
                    if n in (WQ, WK):
                        dst = wT[n][:, c, :].rearrange("p (k d h) -> p k h d", k=C, d=HD)
                        ins = dve.tensor_copy(dst, src[:, c, :].rearrange("p (k h d) -> p k h d", k=C, d=HD))
                    else:
                        ins = dve.tensor_copy(wT[n][:, c, :], src[:, c, :])
                ins.then_inc(set_drained, 1)
                dve.wait_ge(set_drained, n + 2)
                dve.tensor_tensor(squares[n][:, :, :], wT[n][:, :, :], wT[n][:, :, :], ALU.mult).then_inc(sq_ready, 1)
            for n in range(5):
                dve.wait_ge(set_filled, n + 7)
                ps = banks[2 + n % 2][:, 0:C * B].rearrange("p (c b) -> p c b", c=C)
                dve.tensor_scalar(dcoef[n][:, :, :], ps, 1e-8, None, ALU.add).then_inc(set_drained, 1)
            dve.wait_ge(roots_ready, 5)
            dve.tensor_scalar(dcoef[WQ][:, :, :], dcoef[WQ][:, :, :], HD ** -0.5, None, ALU.mult).then_inc(d_ready, 1)
            dve.tensor_tensor(dcoef[WV][:, :, :], dcoef[WV][:, :, :], condT[:, C:2 * C, :], ALU.mult)\
                .then_inc(d_ready, 1)
            dve.wait_ge(d_ready, 3)

            def norm(t, p):
                dve.wait_ge(xs_ready, (t + 1).value)
                for c in range(C):
                    ins = dve.bn_stats(stats[:, c, :], xs[:, c, :])
                ins.then_inc(stats_ready, 1)
                met = ahead(dve, t + 1)
                dve.wait_ge(const_ready, CONSTANTS)
                dve.wait_ge(stats_ready, met)
                for c in range(C):
                    ins = dve.bn_aggr(mv[:, c, :], stats[:, c, :])
                ins.then_inc(aggr_ready, 1)
                dve.wait_ge(aggr_ready, (t + 1).value)
                dve.tensor_scalar(var[:, :], mv[:, :, 1], 1e-5, None, ALU.add).then_inc(var_ready, 1)
                dve.wait_ge(rstd_ready, (t + 1).value)
                for c in range(C):
                    ins = dve.tensor_scalar(xn[:, c, :], xs[:, c, :], mv[:, c, 0:1], rstd[:, c:c + 1],
                                            ALU.subtract, ALU.mult)
                ins.then_inc(xn_ready, 1)

            def rest(t, p, use, n, parts, rst, first, third):
                b = BANK[use]
                dve.wait_ge(first, (t + 1).value)
                dve.wait_ge(third, t.value)
                for c in range(C):
                    ins = dve.scalar_tensor_tensor(out=rst[:, c, :], in0=gen3[b][:, c, :],
                                                   scalar=dcoef[n][:, c, bass.ds(t.value, 1)], in1=parts[:, c, 0, :],
                                                   op0=ALU.mult, op1=ALU.subtract)
                ins.then_inc(drained[b], 1)

            def ev_v(t, p):
                b = BANK["v"]
                dve.wait_ge(av_done, ((t - 1) * 4).value)
                dve.wait_ge(filled[b], uses("v", t).value)
                for c in range(C):
                    ins = dve.tensor_copy(vaug[p][:, c, :, 0:HD], gen3[b][:, c, :].rearrange("p (h d) -> p h d", d=HD))
                ins.then_inc(drained[b], 1)

            def maxima(t, p, h):
                dve.wait_ge(s_filled, (t * H + (h + 1)).value)
                dve.tensor_reduce(mx[:, :, h], sc_ps[h % 2][:, :].rearrange("p (c k) -> p c k", c=C), AX.X, ALU.max)\
                    .then_inc(s_drained, 1)

            def minus_max(t, p):
                b = BANK["maxT"]
                ps = gen[b][0:H, 0:S]
                dve.wait_ge(nm_in, (t * 48).value)
                dve.wait_ge(filled[b], uses("maxT", t).value)
                dve.tensor_scalar(nm[:, 0, :], ps, -1.0, None, ALU.mult).then_inc(n1_ready, 1)
                dve.wait_ge(n1_ready, (t + 1).value)
                dve.scalar_tensor_tensor(out=nrest[:, :], in0=ps, scalar=-1.0, in1=nm[:, 0, :],
                                         op0=ALU.mult, op1=ALU.subtract).then_inc(drained[b], 1)
                dve.wait_ge(drained[b], uses("maxT", t).value)
                dve.tensor_copy(nm[:, 1, :], nrest[:, :]).then_inc(n2_ready, 1)
                dve.wait_ge(n2_ready, (t + 1).value)
                dve.tensor_tensor(nm[:, 2, :], nrest[:, :], nm[:, 1, :], ALU.subtract).then_inc(n3_ready, 1)

            def normalise(t, p, c):
                use = ("o2a", "o2b")[c]
                b = BANK[use]
                ps = gen[b][:, :].rearrange("p (h w) -> p h w", w=VW)
                dve.wait_ge(filled[b], uses(use, t).value)
                dve.reciprocal(rden[:, c, :], ps[:, :, HD]).then_inc(rden_ready, 1)
                dve.wait_ge(rden_ready, (t * 2 + (c + 1)).value)
                dve.tensor_tensor(on[:, c, :].rearrange("p (h d) -> p h d", d=HD), ps[:, :, 0:HD],
                                  rden[:, c, :].unsqueeze(2).to_broadcast([P, H, HD]), ALU.mult)\
                    .then_inc(drained[b], 1)

            def ev_w(t, p):
                b = BANK["w"]
                dve.wait_ge(filled[b], uses("w", t).value)
                dve.wait_ge(drained[BANK["u"]], uses("u", t).value)
                for c in range(C):
                    ins = dve.scalar_tensor_tensor(out=yT[:, c, :], in0=gen3[b][:, c, :],
                                                   scalar=dcoef[WW][:, c, bass.ds(t.value, 1)], in1=skipT[:, c, :],
                                                   op0=ALU.mult, op1=ALU.add)
                ins.then_inc(drained[b], 1)

            def choose(t, p):
                b = BANK["lg"]
                dve.wait_ge(filled[b], uses("lg", t).value)
                dve.tensor_scalar(lg[:, :, :], gen[b][:, 0:C * NE].rearrange("p (c e) -> p c e", c=C), CLAMP, -CLAMP,
                                  ALU.min, ALU.max).then_inc(drained[b], 1)
                met = ahead(dve, uses("lg", t))
                dve.wait_ge(const_ready, CONSTANTS)
                dve.wait_ge(drained[b], met)
                for c in range(C):
                    ins = dve.max(top8[:, c, :], lg[:, c, :])
                ins.then_inc(top_ready, 1)
                met = ahead(dve, t + 1)
                dve.wait_ge(const_ready, CONSTANTS)
                dve.wait_ge(top_ready, met)
                for c in range(C):
                    ins = dve.max_index(idx8[:, c, :], top8[:, c, :], lg[:, c, :])
                ins.then_inc(idx_ready, 1)
                dve.wait_ge(ex_ready, t.value)
                dve.tensor_tensor(gap[:, :], top8[:, :, 1], top8[:, :, 0], ALU.subtract).then_inc(gap_ready, 1)
                dve.wait_ge(idx_ready, (t + 1).value)
                dve.tensor_copy(idxf[:, :, :], idx8[:, :, 0:TOPK]).then_inc(idxf_ready, 1)
                dve.wait_ge(idxf_ready, (t + 1).value)
                for k in range(TOPK):
                    dve.tensor_tensor(onehot[:, :, k, :], expert_no[:, :].unsqueeze(1).to_broadcast([P, C, NE]),
                                      idxf[:, :, k:k + 1].to_broadcast([P, C, NE]), ALU.is_equal)\
                        .then_inc(onehot_ready, 1)
                dve.wait_ge(onehot_ready, (t * 2 + 2).value)
                dve.tensor_tensor(chosen[:, :, :], onehot[:, :, 0, :], onehot[:, :, 1, :], ALU.add)\
                    .then_inc(chosen_ready, 1)

            def route(t, p):
                dve.wait_ge(ex_ready, (t + 1).value)
                dve.tensor_scalar(den[:, :], ex[:, :], 1.0, 1e-12, ALU.add, ALU.add).then_inc(den_ready, 1)
                dve.wait_ge(den_ready, (t * 2 + 1).value)
                dve.reciprocal(pr[:, :, 0], den[:, :]).then_inc(den_ready, 1)
                dve.wait_ge(den_ready, (t * 2 + 2).value)
                dve.tensor_tensor(pr[:, :, 1], ex[:, :], pr[:, :, 0], ALU.mult).then_inc(pr_ready, 1)
                b = BANK["rt"]
                dve.wait_ge(filled[b], uses("rt", t).value)
                ps = gen[b]
                for c in range(C):
                    dve.wait_ge(base_step, (t * 3 + (c + 1)).value)
                    dve.tensor_tensor(base[:, c + 1, :], base[:, c, :], ps[:, (C + c) * NE:(C + c + 1) * NE], ALU.add)\
                        .then_inc(base_step, 1)
                dve.tensor_tensor(pos[:, :, :], ps[:, 0:C * NE].rearrange("p (c e) -> p c e", c=C), base[:, 0:C, :],
                                  ALU.add).then_inc(drained[b], 1)
                dve.wait_ge(drained[b], uses("rt", t).value)
                dve.wait_ge(base_step, (t * 3 + 3).value)
                dve.tensor_copy(base[:, 0, :], base[:, C, :]).then_inc(base_step, 1)
                dve.tensor_scalar(over[:, :, :], pos[:, :, :], float(CAP), FAR, ALU.is_ge, ALU.mult)\
                    .then_inc(over_ready, 1)
                dve.tensor_tensor(place[:, :, :], pos[:, :, :], expert_base[:, :].unsqueeze(1).to_broadcast([P, C, NE]),
                                  ALU.add).then_inc(place_step, 1)
                dve.wait_ge(over_ready, (t + 1).value)
                dve.wait_ge(place_step, (t * 2 + 1).value)
                dve.tensor_tensor(place[:, :, :], place[:, :, :], over[:, :, :], ALU.add).then_inc(place_step, 1)
                dve.wait_ge(place_step, (t * 2 + 2).value)
                for k in range(TOPK):
                    ins = dve.tensor_tensor(picked[:, :, k, :], onehot[:, :, k, :], place[:, :, :], ALU.mult)
                ins.then_inc(picked_ready, 1)
                dve.wait_ge(picked_ready, (t + 1).value)
                dve.tensor_reduce(slot_f[:, :, :], picked[:, :, :, :], AX.X, ALU.add).then_inc(slotf_ready, 1)
                dve.wait_ge(slotf_ready, (t + 1).value)
                dve.wait_ge(entries_out, (t * (C * TOPK * 16)).value)
                dve.tensor_copy(slot_i[:, :, :], slot_f[:, :, :])
                dve.tensor_copy(entry[:, :, :, 0], token_f[:, :].unsqueeze(2).to_broadcast([P, C, TOPK]))\
                    .then_inc(token_read, 1)
                dve.wait_ge(pr_ready, (t + 1).value)
                dve.tensor_copy(entry[:, :, :, 1].bitcast(F32), pr[:, :, :]).then_inc(entry_ready, 1)
                dve.wait_ge(token_read, (t * 2 + 1).value)
                dve.tensor_scalar(token_f[:, :], token_f[:, :], float(S), None, ALU.add).then_inc(token_read, 1)
                dve.wait_ge(token_read, (t * 2 + 2).value)

            def pro():
                for t, p in ((Count(0), 0), (Count(1), 1)):
                    norm(t, p)
                    rest(t, p, "q", WQ, qparts, qrest, q1_ready, q3_ready)
                    rest(t, p, "k", WK, kparts, krest, k1_ready, k3_ready)
                    if p == 0:
                        ev_v(t, p)
                for h in range(H):
                    maxima(Count(0), 0, h)
                minus_max(Count(0), 0)
                norm(Count(2), 0)

            def slot(s, p):
                for i in range(H + LAG):
                    if i < H and has(s, 1):
                        maxima(s + 1, 1 - p, i)
                    if i == 1 and has(s, -1):
                        normalise(s - 1, 1 - p, 0)
                    if i == 2 and has(s, -1):
                        normalise(s - 1, 1 - p, 1)
                    if i == 3 and has(s, 2):
                        rest(s + 2, p, "q", WQ, qparts, qrest, q1_ready, q3_ready)
                    if i == 4 and has(s, 2):
                        rest(s + 2, p, "k", WK, kparts, krest, k1_ready, k3_ready)
                    if i == 7 and has(s, -1):
                        ev_w(s - 1, 1 - p)
                    if i == 9 and has(s, -1):
                        choose(s - 1, 1 - p)
                    if i == 13 and has(s, -1):
                        route(s - 1, 1 - p)
                    if i == 14 and has(s, 1):
                        ev_v(s + 1, 1 - p)
                    if i == 15 and has(s, 1):
                        minus_max(s + 1, 1 - p)
                    if i == 16 and has(s, 3):
                        norm(s + 3, 1 - p)
                for n in range(PIECES):
                    if s.i is None and s.first == B - 2 + n // 2:
                        split_low(Count(0), 0, n)

            def split_low(e, p, n):
                dve.wait_ge(w_hi_ready, (e * PIECES + (n + 1)).value)
                dve.tensor_tensor(piece(w_lo[p], n), piece(w_raw, n), piece(w_hi[p], n), ALU.subtract)\
                    .then_inc(w_lo_ready, 1)

            def take_low(nb):
                for c in range(C):
                    dve.wait_ge(xeT_hi_ready, (nb * C + (c + 1)).value)
                    dve.tensor_tensor(xeT_lo[:, c, :], gen[c][:, :], xeT_hi[:, c, :], ALU.subtract)\
                        .then_inc(xeT_lo_ready, 1)

            def hidden_low(nb, f):
                dve.wait_ge(h_hi_ready, (nb * FC + (f + 1)).value)
                dve.tensor_tensor(hid_lo[:, f, :], hid[f % 2][:, :], hid_hi[:, f, :], ALU.subtract)\
                    .then_inc(h_lo_ready, 1)

            def blocks(i, more):
                for j in range(2 * NBLK):
                    nb = at(i, j)
                    for f in range(FC):
                        dve.wait_ge(sg_ready, (nb * FC + (f + 1)).value)
                        if f >= 2:
                            dve.wait_ge(h_lo_ready, (nb * FC + (f - 1)).value)
                        dve.tensor_tensor(hid[f % 2][:, :], sg[f % 2][:, :], banks[4 + f % 2][:, :], ALU.mult)\
                            .then_inc(h_ready, 1)
                        if f >= 1:
                            hidden_low(nb, f - 1)
                    hidden_low(nb, FC - 1)
                    if more or j < 2 * NBLK - 1:
                        take_low(nb + 1)
                    e, these = pieces_at(i, j)
                    for n in these:
                        split_low(e, 1 - j // NBLK, n)
                    dve.wait_ge(down_filled, (nb * 2 + 1).value)
                    if last_one(i, j):
                        dve.wait_ge(adds_out, (nb * (JT * 16)).value)
                    for tt in (0, 1):
                        ins = dve.tensor_scalar(ye[:, tt, :], o_ps[0][:, tt * D:(tt + 1) * D],
                                                tab[j % 2][:, tt, 1:2].bitcast(F32), None, ALU.mult)
                    ins.then_inc(ye_dve, 1)

            def last():
                take_low(Count(0))
                with dve.Fori(0, NE // 2 - 1) as i:
                    blocks(i, True)
                blocks(NE // 2 - 1, False)

            slots_of(dve, pro, slot, last)

        @block.tensor
        def _(pe):
            pe.wait_ge(const_ready, CONSTANTS)
            pe.wait_ge(small_in, 32)
            for c in range(4):
                ins = pe.transpose(banks[2][:, c * B:(c + 1) * B], cond_sb[:, c * P:(c + 1) * P], ident[0:B, 0:B])
            ins.then_inc(set_filled, 1)
            pe.wait_ge(w_in, 5 * 16)
            for n in range(5):
                pe.wait_ge(set_drained, n)
                for ic in range(C):
                    for oc in range(C):
                        ins = pe.transpose(banks[2 + (n + 1) % 2][:, ic * D + oc * P:ic * D + (oc + 1) * P],
                                           wload[n][:, oc, ic * P:(ic + 1) * P], ident[:, :])
                ins.then_inc(set_filled, 1)
            for n in range(5):
                pe.wait_ge(set_drained, n + 5)
                pe.wait_ge(sq_ready, n + 2)
                side = 0 if n < 3 else C
                for oc in range(C):
                    for ic in range(C):
                        ins = pe.matmul(banks[2 + n % 2][:, oc * B:(oc + 1) * B], squares[n][:, ic, oc * P:(oc + 1) * P],
                                        condsq[:, side + ic, :], start=(ic == 0), stop=(ic == C - 1))
                ins.then_inc(set_filled, 1)

            def begin(use, t):
                b = BANK[use]
                pe.wait_ge(drained[b], (uses(use, t) - 1).value)
                return b

            def transposes(dst, src):
                for a in range(C):
                    for c in range(C):
                        ins = pe.transpose(dst[:, a, c * P:(c + 1) * P], src[:, c, a * P:(a + 1) * P], ident[:, :])
                return ins

            def project(b, w, src):
                for m in range(C):
                    for k in range(C):
                        ins = pe.matmul(gen3[b][:, m, :], w[:, k, m * P:(m + 1) * P], src[:, k, :],
                                        start=(k == 0), stop=(k == C - 1))
                ins.then_inc(filled[b], 1)

            def a_xT(t, p):
                b = begin("xT", t)
                pe.wait_ge(xn_ready, (t + 1).value)
                transposes(gen3[b], xn).then_inc(filled[b], 1)

            def a_proj(t, p, use, n):
                pe.wait_ge(drained[BANK["xT"]], uses("xT", t).value)
                project(begin(use, t), wT[n], xT)

            def a_v(t, p):
                b = begin("v", t)
                pe.wait_ge(drained[BANK["vT"]], uses("vT", t).value)
                transposes(gen3[b], vT[p]).then_inc(filled[b], 1)

            def scores(t, p, h):
                if h % HG == 0:
                    pe.wait_ge(stack_in[h // HG][p], (t * (8 * STACK_LOADS) + (16 - 8 * p) * STACK_LOADS).value)
                pe.wait_ge(s_drained, (t * H + (h - 1)).value)
                for c in range(C):
                    ins = pe.matmul(sc_ps[h % 2][:, c * S:(c + 1) * S], qst[p][0:KS, h, c * P:(c + 1) * P],
                                    kst[p][0:KS, h, :], start=True, stop=True)
                ins.then_inc(s_filled, 1)

            def max_t(t, p):
                b = begin("maxT", t)
                pe.wait_ge(s_drained, (t * H + H).value)
                for c in range(C):
                    ins = pe.transpose(gen[b][0:H, c * P:(c + 1) * P], mx[:, c, :], ident[:, :])
                ins.then_inc(filled[b], 1)

            def shifted(t, p, h):
                if h == 0:
                    pe.wait_ge(nm_in, (t * 48 + 48).value)
                pe.wait_ge(p_ready, (t * H + (h - 1 if h >= 2 else 0)).value)
                for c in range(C):
                    ins = pe.matmul(st_ps[h % 2][:, c * S:(c + 1) * S], kst[p][:, h, c * P:(c + 1) * P],
                                    qst[p][:, h, :], start=True, stop=True)
                ins.then_inc(t_filled, 1)

            def values(t, p, g):
                if g == 0:
                    pe.wait_ge(o_drained, (t * 2).value)
                pe.wait_ge(p_ready, (t * H + (4 * g + 4)).value)
                for c in range(C):
                    for j in range(4):
                        h = 4 * g + j
                        ins = pe.matmul(o_ps[g // 2][VW * j:VW * (j + 1), (g % 2) * S:(g % 2 + 1) * S],
                                        vaug[p][:, c, h, :], probs[h % 8][:, c, :], start=(c == 0), stop=(c == C - 1),
                                        skip_group_check=True)
                ins.then_inc(av_done, 1)

            def d_o2(t, p, c):
                use = ("o2a", "o2b")[c]
                b = begin(use, t)
                pe.wait_ge(o_drained, (t * 2 + 2).value)
                for g in range(4):
                    ins = pe.transpose(gen[b][:, g * P:(g + 1) * P], oTa[:, g, c * P:(c + 1) * P], ident[:, :])
                ins.then_inc(filled[b], 1)

            def d_oT(t, p):
                b = begin("oT", t)
                pe.wait_ge(drained[BANK["o2a"]], uses("o2a", t).value)
                pe.wait_ge(drained[BANK["o2b"]], uses("o2b", t).value)
                transposes(gen3[b], on).then_inc(filled[b], 1)

            def d_w(t, p):
                b = begin("w", t)
                pe.wait_ge(drained[BANK["oT"]], uses("oT", t).value)
                project(b, wT[WW], oT)

            def d_u(t, p):
                project(begin("u", t), wT[WU], vT[p])

            def d_y(t, p):
                b = begin("y", t)
                pe.wait_ge(drained[BANK["w"]], uses("w", t).value)
                transposes(gen3[b], yT).then_inc(filled[b], 1)

            def d_lg(t, p):
                b = begin("lg", t)
                pe.wait_ge(drained[BANK["w"]], uses("w", t).value)
                for c in range(C):
                    for k in range(C):
                        ins = pe.matmul(gen[b][:, c * NE:(c + 1) * NE], yT[:, k, c * P:(c + 1) * P], wr_sb[:, k, :],
                                        start=(k == 0), stop=(k == C - 1))
                ins.then_inc(filled[b], 1)

            def r_counts(t, p):
                b = begin("rt", t)
                pe.wait_ge(chosen_ready, (t + 1).value)
                pe.matmul(gen[b][:, 0:C * NE], before[:, :], chosen[:, :, :].rearrange("p c e -> p (c e)"),
                          start=True, stop=True)
                pe.matmul(gen[b][:, C * NE:2 * C * NE], ones[:, :], chosen[:, :, :].rearrange("p c e -> p (c e)"),
                          start=True, stop=True).then_inc(filled[b], 1)

            def pro():
                pe.wait_ge(d_ready, 3)
                for t, p in ((Count(0), 0), (Count(1), 1)):
                    a_xT(t, p)
                    a_proj(t, p, "q", WQ)
                    a_proj(t, p, "k", WK)
                    a_proj(t, p, "vT", WV)
                    if p == 0:
                        a_v(t, p)
                for h in range(H):
                    scores(Count(0), 0, h)
                max_t(Count(0), 0)

            def slot(s, p):
                for i in range(H + LAG):
                    if i < H and has(s, 1):
                        scores(s + 1, 1 - p, i)
                    if i >= LAG and has(s, 0):
                        shifted(s, p, i - LAG)
                    if i in (9, 13, 17, 19) and has(s, 0):
                        values(s, p, {9: 0, 13: 1, 17: 2, 19: 3}[i])
                    if i == 0 and has(s, 2):
                        a_xT(s + 2, p)
                    if i == 1 and has(s, -1):
                        d_o2(s - 1, 1 - p, 0)
                    if i == 2 and has(s, -1):
                        d_o2(s - 1, 1 - p, 1)
                    if i == 2 and has(s, 2):
                        a_proj(s + 2, p, "q", WQ)
                    if i == 3 and has(s, 2):
                        a_proj(s + 2, p, "k", WK)
                    if i == 4 and has(s, -1):
                        d_oT(s - 1, 1 - p)
                    if i == 6 and has(s, -1):
                        d_w(s - 1, 1 - p)
                    if i == 8 and has(s, -1):
                        d_lg(s - 1, 1 - p)
                    if i == 9 and has(s, -1):
                        d_y(s - 1, 1 - p)
                    if i == 10 and has(s, 0):
                        d_u(s, p)
                    if i == 11 and has(s, 2):
                        a_proj(s + 2, p, "vT", WV)
                    if i == 12 and has(s, -1):
                        r_counts(s - 1, 1 - p)
                    if i == 13 and has(s, 1):
                        a_v(s + 1, 1 - p)
                    if i == 15 and has(s, 1):
                        max_t(s + 1, 1 - p)

            def turn(nb, half, b):
                pe.wait_ge(xeT_lo_ready, (nb * C).value)
                pe.wait_ge(xe_in[b], ((half + 1) * (JT * 16)).value)
                for c in range(C):
                    for j in range(JT):
                        ins = pe.transpose(gen[c][:, j * P:(j + 1) * P], xe[b][:, j, c * P:(c + 1) * P], ident[:, :])
                    ins.then_inc(xeT_filled, 1)

            def halves(dst, st_hi, st_lo, mv_hi, mv_lo, start, stop):
                pe.matmul(dst, st_lo, mv_hi, start=start, stop=False)
                pe.matmul(dst, st_hi, mv_lo, start=False, stop=False)
                return pe.matmul(dst, st_hi, mv_hi, start=False, stop=stop)

            def up(nb, e):
                pe.wait_ge(xeT_lo_ready, (nb * C + C).value)
                for f in range(FC):
                    if f >= 2:
                        pe.wait_ge(h_ready, (nb * FC + (f - 1)).value)
                    for n, bank in ((0, banks[2 + f % 2]), (1, banks[4 + f % 2])):
                        for c in range(C):
                            at_f = c * F + f * P
                            ins = halves(bank[:, :], w_hi[e][:, n, at_f:at_f + P], w_lo[e][:, n, at_f:at_f + P],
                                         xeT_hi[:, c, :], xeT_lo[:, c, :], c == 0, c == C - 1)
                    ins.then_inc(up_filled, 1)

            def down(nb, e):
                for tt in range(JT):
                    for f in range(FC):
                        if tt == 0:
                            pe.wait_ge(h_lo_ready, (nb * FC + (f + 1)).value)
                        ins = halves(o_ps[tt // 2][:, (tt % 2) * D:(tt % 2 + 1) * D],
                                     hid_hi[:, f, tt * P:(tt + 1) * P], hid_lo[:, f, tt * P:(tt + 1) * P],
                                     w_hi[e][:, 2, f * D:(f + 1) * D], w_lo[e][:, 2, f * D:(f + 1) * D],
                                     f == 0, f == FC - 1)
                    if tt % 2:
                        ins.then_inc(down_filled, 1)

            def blocks(i, more):
                for j in range(2 * NBLK):
                    nb = at(i, j)
                    if j % NBLK == 0:
                        e = Count(2 * i + j // NBLK) if isinstance(i, int) else Count(j // NBLK, 2, i)
                        pe.wait_ge(w_lo_ready, (e * PIECES + PIECES).value)
                    up(nb, j // NBLK)
                    half = Count(i * NBLK + (j + 1) // 2) if isinstance(i, int) else Count((j + 1) // 2, NBLK, i)
                    if more or j < 2 * NBLK - 1:
                        turn(nb + 1, half, (j + 1) % 2)
                    down(nb, j // NBLK)

            def last():
                for b in (0, 1):
                    pe.wait_ge(drained[b], BANK_TOTAL[b])
                turn(Count(0), Count(0), 0)
                with pe.Fori(0, NE // 2 - 1) as i:
                    blocks(i, True)
                blocks(NE // 2 - 1, False)

            slots_of(pe, pro, slot, last)


_INS = ["x", "cond_2048", "L0_cond_q_weight", "L0_cond_k_weight", "L0_cond_v_weight", "L0_cond_w_weight",
        "L0_cond_u_weight", "L0_ffn_Wr", "L0_ffn_W1", "L0_ffn_W3", "L0_ffn_W2"]


def kernel(**inputs):
    import numpy as _np
    import concourse.bacc as _bacc
    from concourse import mybir as _mybir
    from concourse.bass_utils import run_bass_kernel_spmd as _run

    nc = _bacc.Bacc("TRN2", target_bir_lowering=False, num_devices=1)
    arrays, args = {}, []
    for name in _INS:
        a = _np.ascontiguousarray(inputs[name])
        arrays[f"in_{name}"] = a
        args.append(nc.dram_tensor(f"in_{name}", a.shape, _mybir.dt.from_np(a.dtype), kind="ExternalInput").ap())
    out = nc.dram_tensor("out_x", (B, S, D), _mybir.dt.from_np(_np.dtype("float32")), kind="ExternalOutput").ap()
    adaln_moe(nc, *args, out)
    r = _run(nc, [arrays], core_ids=[0])
    return r.results[0]["out_x"]
```

```python
from contextlib import ExitStack

import numpy as np

import concourse.bass as bass
from concourse import mybir

ALU = mybir.AluOpType
ACT = mybir.ActivationFunctionType
AX = mybir.AxisListType
F32 = mybir.dt.float32
F32R = mybir.dt.float32r
BF16 = mybir.dt.bfloat16
I32 = mybir.dt.int32
U32 = mybir.dt.uint32

P = 128
B, S, D = 32, 256, 256
H, HD = 16, 16
NE, F, TOPK = 8, 1024, 2
T = B * S
CAP = -(-T * TOPK * 5 // (4 * NE))
C = D // P
FC = F // P
BLK = 512
JT = BLK // P
NBLK = CAP // BLK
PIECES = 6
PIECE = 3 * C * F // PIECES
assert NBLK * BLK == CAP and S == D == C * P
CONSTANTS = 9
TWO_ONES = float(np.array(0x3F803F80, np.uint32).view(np.float32))
CLAMP = 10000.0
FAR = 65536.0
Q_RUNS = ((0, 3, 0, False), (3, 2, 0, False), (5, 1, 0, False))
K_RUNS = ((0, 3, 0, True), (3, 2, 1, True), (5, 1, 2, True))
KS = HD * 6
KM = KS + 3
STACK_LOADS = sum(pairs if same else 1 for _, pairs, _, same in Q_RUNS + K_RUNS)
HG = H // C
LAG = 4
VW = 32

BANK = {"xT": 0, "o2a": 1, "o2b": 0, "q": 1, "k": 0, "oT": 1, "w": 0, "lg": 1, "y": 0, "u": 1,
        "v": 0, "maxT": 1, "rt": 1, "vT": 0}
SLOT_USES = (("xT", 2), ("o2a", -1), ("o2b", -1), ("q", 2), ("k", 2), ("oT", -1), ("w", -1), ("lg", -1),
             ("y", -1), ("u", 0), ("v", 1), ("maxT", 1), ("rt", -1), ("vT", 2))
PRO_USES = (("xT", 0), ("q", 0), ("k", 0), ("vT", 0), ("v", 0), ("xT", 1), ("q", 1), ("k", 1), ("vT", 1), ("maxT", 0))


def bank_counts():
    n, at = [0, 0], {}

    def use(name, t):
        n[BANK[name]] += 1
        at[name, t] = n[BANK[name]]

    for name, t in PRO_USES:
        use(name, t)
    for s in range(B + 1):
        for name, ahead_by in SLOT_USES:
            if 0 <= s + ahead_by < B:
                use(name, s + ahead_by)
    return at, n


COUNTS, BANK_TOTAL = bank_counts()


class Count:

    def __init__(self, first, step=0, i=None):
        self.first, self.step, self.i = first, step, i

    def __add__(self, n):
        return Count(self.first + n, self.step, self.i)

    def __sub__(self, n):
        return self + -n

    def __mul__(self, n):
        return Count(self.first * n, self.step * n, self.i)

    @property
    def value(self):
        return max(self.first, 0) if self.i is None else self.i * self.step + self.first


def uses(name, t):
    if t.i is None:
        return Count(COUNTS[name, t.first])
    at = [COUNTS[name, t.first + n * t.step] for n in (1, 2, 3)]
    assert at[2] - at[1] == at[1] - at[0]
    return Count(2 * at[0] - at[1], at[1] - at[0], t.i)


def ahead(eng, count):
    return count.value if count.i is None else eng.compute_val(count.value)


def adaln_moe(nc, x, cond, wq, wk, wv, ww, wu, wr, w1, w3, w2, out):
    with ExitStack() as ctx:
        phase = ctx.enter_context(ExitStack())

        def sb(name, shape, dt=F32):
            return ctx.enter_context(nc.sbuf_tensor(name, shape, dt))

        def sb_attention(name, shape, dt=F32):
            return phase.enter_context(nc.sbuf_tensor(name, shape, dt))

        def pb(name):
            return ctx.enter_context(nc.psum_tensor(name, [P, 512], F32))

        def sem(name):
            return ctx.enter_context(nc.semaphore(name))

        y_rows = nc.dram_tensor("y_rows", [T, D], F32, kind="Internal").ap()
        slots = nc.dram_tensor("slot_table", [NE * CAP, 2], I32, kind="Internal").ap()
        parts_rows = nc.dram_tensor("parts_rows", [2, 2, C, 3, P, S], BF16, kind="Internal").ap()
        x_rows = x.rearrange("b s d -> (b s) d")
        out_rows = out.rearrange("b s d -> (b s) d")

        ident = sb("ident", [P, P])
        before = sb("before", [P, P], BF16)
        ones = sb("ones", [P, P], BF16)
        expert_no = sb("expert_no", [P, NE])
        expert_no_i = sb("expert_no_i", [P, NE], I32)
        expert_base = sb("expert_base", [P, NE])
        token_no = sb("token_no", [P, C], I32)
        token_f = sb("token_f", [P, C])
        w_raw = sb("w_raw", [P, 3, C * F])
        w_hi0 = sb("w_hi0", [P, 3, C * F], F32R)
        w_lo0 = sb("w_lo0", [P, 3, C * F], F32R)
        tab = [sb(f"tab{p}", [P, JT, 2], I32) for p in (0, 1)]
        xe = [sb(f"xe{p}", [P, JT, D]) for p in (0, 1)]
        ww_T = sb_attention("ww_T", [P, C, D])
        wu_T = sb_attention("wu_T", [P, C, D])
        wT_hi = [sb_attention(f"wT_hi{n}", [P, C, D], F32R) for n in range(3)]
        wT_lo = [sb_attention(f"wT_lo{n}", [P, C, D], F32R) for n in range(3)]
        wr_sb = sb_attention("wr_sb", [P, C, NE])
        condT = sb_attention("condT", [P, 4, B])
        condsq = sb_attention("condsq", [P, 4, B])
        dcoef_all = sb_attention("dcoef", [P, 5, C, B])
        dcoef = [dcoef_all[:, n, :, :] for n in range(5)]
        x_tok = [sb_attention(f"x_tok{p}", [P, C, D]) for p in (0, 1)]
        s1_all = [sb_attention(f"s1_all{p}", [P, D]) for p in (0, 1)]
        xs = sb_attention("xs", [P, C, D])
        stats = sb_attention("stats", [P, C, 6])
        mv = sb_attention("mv", [P, C, 2])
        var = sb_attention("var", [P, C])
        rstd = sb_attention("rstd", [P, C])
        minus_half = sb_attention("minus_half", [P, C])
        xn = sb_attention("xn", [P, C, D])
        xT_hi = sb_attention("xT_hi", [P, C, S], F32R)
        xT_lo = sb_attention("xT_lo", [P, C, S], F32R)
        qparts = sb_attention("qparts", [P, C, 3, S], BF16)
        kparts = sb_attention("kparts", [P, C, 3, S], BF16)
        qrest = sb_attention("qrest", [P, C, S])
        krest = sb_attention("krest", [P, C, S])
        vT = [sb_attention(f"vT{p}", [P, C, S]) for p in (0, 1)]
        vaug = [sb_attention(f"vaug{p}", [P, C, H, VW]) for p in (0, 1)]
        qst = [sb_attention(f"qst{p}", [P, H, S], BF16) for p in (0, 1)]
        kst = [sb_attention(f"kst{p}", [P, H, S], BF16) for p in (0, 1)]
        mx = sb_attention("mx", [P, C, H])
        nm = sb_attention("nm", [H, 3, S], BF16)
        nrest = sb_attention("nrest", [H, S])
        probs = [sb_attention(f"probs{n}", [P, C, S]) for n in range(8)]
        wload = probs
        oTa = sb_attention("oTa", [P, 4, S])
        rden = sb_attention("rden", [P, C, H])
        on = sb_attention("on", [P, C, D])
        oT = sb_attention("oT", [P, C, S])
        skipT = sb_attention("skipT", [P, C, S])
        yT = sb_attention("yT", [P, C, S])
        y_tok = sb_attention("y_tok", [P, C, D])
        lg = sb_attention("lg", [P, C, NE])
        top8 = sb_attention("top8", [P, C, 8])
        idx8 = sb_attention("idx8", [P, C, 8], U32)
        idxf = sb_attention("idxf", [P, C, TOPK])
        onehot = sb_attention("onehot", [P, C, TOPK, NE])
        chosen = sb_attention("chosen", [P, C, NE], BF16)
        gap = sb_attention("gap", [P, C])
        ex = sb_attention("ex", [P, C])
        den = sb_attention("den", [P, C])
        pr = sb_attention("pr", [P, C, TOPK])
        base = sb_attention("base", [P, C + 1, NE])
        pos = sb_attention("pos", [P, C, NE])
        over = sb_attention("over", [P, C, NE])
        place = sb_attention("place", [P, C, NE])
        picked = sb_attention("picked", [P, C, TOPK, NE])
        slot_f = sb_attention("slot_f", [P, C, TOPK])
        slot_i = sb_attention("slot_i", [P, C, TOPK], U32)
        entry = sb_attention("entry", [P, C, TOPK, 2], I32)
        squares = [probs[5], probs[6], probs[7], xn, on]
        wT = [vT[0], vT[1], yT, ww_T, wu_T]
        o_rows = oTa[:, :, :].rearrange("p g s -> p (g s)")
        empty = o_rows[:, 0:2 * NE * CAP // P].bitcast(I32).rearrange("p (n w) -> p n w", w=2)
        cond_sb = o_rows[0:B, 2 * S:2 * S + 2 * D]
        dsum = y_tok[:, :, :].rearrange("p c d -> p (c d)")[:, 0:5 * C * B].rearrange("p (n c b) -> p n c b", n=5, c=C)
        dwork = qrest[:, :, :].rearrange("p c d -> p (c d)")[:, 0:5 * C * B].rearrange("p (n c b) -> p n c b", n=5, c=C)
        phase.close()

        w_hi = [w_hi0, sb("w_hi1", [P, 3, C * F], F32R)]
        w_lo = [w_lo0, sb("w_lo1", [P, 3, C * F], F32R)]
        xeT_hi = sb("xeT_hi", [P, C, BLK], F32R)
        xeT_lo = sb("xeT_lo", [P, C, BLK], F32R)
        sg = [sb(f"sg{p}", [P, BLK]) for p in (0, 1)]
        hid = [sb(f"hid{p}", [P, BLK]) for p in (0, 1)]
        hid_hi = sb("hid_hi", [P, FC, BLK], F32R)
        hid_lo = sb("hid_lo", [P, FC, BLK], F32R)
        ye = sb("ye", [P, JT, D])

        banks = [pb(f"bank{n}") for n in range(8)]
        gen = banks[0:2]
        sc_ps = banks[2:4]
        st_ps = banks[4:6]
        o_ps = banks[6:8]
        gen3 = [g[:, :].rearrange("p (c n) -> p c n", c=C) for g in gen]

        filled = [sem(f"bank{n}_filled") for n in (0, 1)]
        drained = [sem(f"bank{n}_drained") for n in (0, 1)]
        w_in = sem("w_in")
        small_in = sem("small_in")
        const_ready = sem("const_ready")
        const_step = sem("const_step")
        rows_zero = sem("rows_zero")
        set_filled = sem("set_filled")
        set_drained = sem("set_drained")
        sq_ready = sem("sq_ready")
        numbers_ready = sem("numbers_ready")
        wT_hi_ready = sem("wT_hi_ready")
        wT_lo_ready = sem("wT_lo_ready")
        roots_ready = sem("roots_ready")
        newton_step = sem("newton_step")
        ident_ready = sem("ident_ready")
        rows_ready = sem("rows_ready")
        d_ready = sem("d_ready")
        table_empty = sem("table_empty")
        out_is_x = sem("out_is_x")
        x_in = [sem(f"x_in{p}") for p in (0, 1)]
        xs_ready = sem("xs_ready")
        stats_ready = sem("stats_ready")
        aggr_ready = sem("aggr_ready")
        var_ready = sem("var_ready")
        rstd_ready = sem("rstd_ready")
        xn_ready = sem("xn_ready")
        xT_hi_ready = sem("xT_hi_ready")
        q1_ready = sem("q1_ready")
        k1_ready = sem("k1_ready")
        q2_ready = sem("q2_ready")
        k2_ready = sem("k2_ready")
        q3_ready = sem("q3_ready")
        k3_ready = sem("k3_ready")
        parts_out = [sem(f"{n}_parts_out") for n in "qk"]
        stack_in = [[sem(f"stack{half}_in{p}") for p in (0, 1)] for half in range(C)]
        s_filled = sem("s_filled")
        s_drained = sem("s_drained")
        n1_ready = sem("n1_ready")
        n2_ready = sem("n2_ready")
        n3_ready = sem("n3_ready")
        nm_in = sem("nm_in")
        t_filled = sem("t_filled")
        p_ready = sem("p_ready")
        av_done = sem("av_done")
        o_drained = sem("o_drained")
        rden_ready = sem("rden_ready")
        y_out = sem("y_out")
        top_ready = sem("top_ready")
        idx_ready = sem("idx_ready")
        idxf_ready = sem("idxf_ready")
        onehot_ready = sem("onehot_ready")
        chosen_ready = sem("chosen_ready")
        gap_ready = sem("gap_ready")
        ex_ready = sem("ex_ready")
        den_ready = sem("den_ready")
        pr_ready = sem("pr_ready")
        base_step = sem("base_step")
        pos_ready = sem("pos_ready")
        over_ready = sem("over_ready")
        place_step = sem("place_step")
        picked_ready = sem("picked_ready")
        slotf_ready = sem("slotf_ready")
        token_read = sem("token_read")
        entry_ready = sem("entry_ready")
        entries_out = sem("entries_out")
        w_raw_in = sem("w_raw_in")
        w_hi_ready = sem("w_hi_ready")
        w_lo_ready = sem("w_lo_ready")
        tab_in = sem("tab_in")
        xe_zero = sem("xe_zero")
        xe_in = [sem(f"xe_in{p}") for p in (0, 1)]
        xeT_filled = sem("xeT_filled")
        xeT_hi_ready = sem("xeT_hi_ready")
        xeT_lo_ready = sem("xeT_lo_ready")
        up_filled = sem("up_filled")
        sg_ready = sem("sg_ready")
        h_ready = sem("h_ready")
        h_hi_ready = sem("h_hi_ready")
        h_lo_ready = sem("h_lo_ready")
        down_filled = sem("down_filled")
        ye_act = sem("ye_act")
        ye_dve = sem("ye_dve")
        adds_out = sem("adds_out")

        weights = (wq, wk, wv, ww, wu)
        WQ, WK, WV, WW, WU = range(5)

        block = ctx.enter_context(nc.Block())

        def at(i, j):
            return Count(i * 2 * NBLK + j) if isinstance(i, int) else Count(j, 2 * NBLK, i)

        def piece(w, n):
            return w[:, n // 2, (n % 2) * PIECE:(n % 2 + 1) * PIECE]

        def pieces_at(i, j):
            if j % NBLK not in (1, 2, 3) or (isinstance(i, int) and j >= NBLK):
                return None, ()
            p, n = j // NBLK, 2 * (j % NBLK - 1)
            return (Count(2 * i + p + 1) if isinstance(i, int) else Count(p + 1, 2, i)), (n, n + 1)

        def last_one(i, j):
            return isinstance(i, int) and j == 2 * NBLK - 1

        def has(s, ahead_by):
            return s.i is not None or 0 <= s.first + ahead_by < B

        def slots_of(eng, pro, slot, last):
            pro()
            for s in (0, 1, 2):
                slot(Count(s), s % 2)
            with eng.Fori(1, (B - 4) // 2) as i:
                slot(Count(1, 2, i), 1)
                slot(Count(2, 2, i), 0)
            for s in range(B - 3, B + 1):
                slot(Count(s), s % 2)
            last()

        @block.sync
        def _(sp):
            for n, w in enumerate(weights):
                sp.dma_start(wload[n][:, :, :], w.rearrange("(c p) i -> p c i", p=P)).then_inc(w_in, 16)
            sp.dma_start(cond_sb[:, :], cond).then_inc(small_in, 16)
            sp.dma_start(wr_sb[:, :, :], wr.rearrange("(c p) e -> p c e", p=P)).then_inc(small_in, 16)

            def load_x(t, p):
                met = ahead(sp, t - 1)
                sp.wait_ge(const_ready, CONSTANTS)
                sp.wait_ge(xs_ready, met)
                sp.dma_start(x_tok[p][:, :, :], x[bass.ds(t.value, 1), :, :].rearrange("b (c p) d -> p (b c) d", p=P))\
                    .then_inc(x_in[p], 16)
                sp.dma_start(s1_all[p][:, :], cond[bass.ds(t.value, 1), 0:D].to_broadcast([P, D])).then_inc(x_in[p], 16)

            def store_parts(t, p):
                for n, (parts, first, third) in enumerate(((qparts, q1_ready, q3_ready), (kparts, k1_ready, k3_ready))):
                    sp.wait_ge(first, (t + 1).value)
                    sp.wait_ge(third, (t + 1).value)
                    sp.dma_start(parts_rows[n, p].rearrange("c n m s -> m c n s"), parts[:, :, :, :])\
                        .then_inc(parts_out[n], 16)

            def load_stack(t, p, half):
                met = ahead(sp, t * 16 + 16)
                sp.wait_ge(const_ready, CONSTANTS)
                sp.wait_ge(parts_out[0], met)
                sp.wait_ge(parts_out[1], (t * 16 + 16).value)
                sp.wait_ge(t_filled, ((t - 2) * H + HG * (half + 1)).value)
                for n, st, runs in ((0, qst, Q_RUNS), (1, kst, K_RUNS)):
                    for row, pairs, part, same in runs:
                        src = parts_rows[n, p, half, part:part + (1 if same else pairs)]\
                            .rearrange("n (d h) s -> (n d) (h s)", h=HG)
                        for r in range(pairs if same else 1):
                            rows = slice((row + r) * HD, (row + (r + 1 if same else pairs)) * HD)
                            sp.dma_start(st[p][rows, half * HG:(half + 1) * HG, :].rearrange("r h s -> r (h s)"), src)\
                                .then_inc(stack_in[half][p], 16)

            def max_rows(t, p):
                met = ahead(sp, t + 1)
                sp.wait_ge(const_ready, CONSTANTS)
                sp.wait_ge(n3_ready, met)
                sp.wait_ge(t_filled, ((t - 1) * H).value)
                for n in range(3):
                    sp.dma_start(qst[p][KS + n:KS + n + 1, :, :], nm[:, n, :]).then_inc(nm_in, 16)

            def store_y(t, p):
                met = ahead(sp, uses("y", t))
                sp.wait_ge(const_ready, CONSTANTS)
                sp.wait_ge(drained[BANK["y"]], met)
                sp.dma_start(y_rows[bass.ds((t * S).value, S), :].rearrange("(c p) d -> p c d", p=P), y_tok[:, :, :])\
                    .then_inc(y_out, 16)

            def load_expert(e):
                for n, src in enumerate((w1, w3)):
                    sp.dma_start(w_raw[:, n, :].rearrange("p (c f) -> p c f", c=C),
                                 src[bass.ds(e.value, 1), :, :].rearrange("e (c p) f -> p (e c) f", p=P))\
                        .then_inc(w_raw_in, 16)
                sp.dma_start(w_raw[:, 2, :].rearrange("p (c d) -> p c d", c=FC),
                             w2[bass.ds(e.value, 1), :, :].rearrange("e (c p) d -> p (e c) d", p=P))\
                    .then_inc(w_raw_in, 16)

            def pro():
                load_x(Count(0), 0)
                load_x(Count(1), 1)
                store_parts(Count(0), 0)
                load_stack(Count(0), 0, 0)
                load_stack(Count(0), 0, 1)
                load_x(Count(2), 0)
                store_parts(Count(1), 1)
                load_stack(Count(1), 1, 0)
                sp.wait_ge(rows_ready, 4)
                max_rows(Count(0), 0)
                load_stack(Count(1), 1, 1)

            def copy_x(t):
                sp.dma_start(out[bass.ds(t.value, 1), :, :].rearrange("b (q r) d -> (b q) (r d)", q=16),
                             x[bass.ds(t.value, 1), :, :].rearrange("b (q r) d -> (b q) (r d)", q=16))\
                    .then_inc(out_is_x, 16)

            def slot(s, p):
                if has(s, 3):
                    load_x(s + 3, 1 - p)
                if has(s, 2):
                    store_parts(s + 2, p)
                if has(s, -1):
                    store_y(s - 1, 1 - p)
                if has(s, 2):
                    load_stack(s + 2, p, 0)
                if has(s, 1):
                    max_rows(s + 1, 1 - p)
                if has(s, 2):
                    load_stack(s + 2, p, 1)
                if has(s, 0):
                    copy_x(s)
                if s.i is None and s.first == B - 3:
                    load_expert(Count(0))

            def last():
                with sp.Fori(1, NE) as i:
                    e = Count(0, 1, i)
                    met = ahead(sp, e * PIECES)
                    sp.wait_ge(const_ready, CONSTANTS)
                    sp.wait_ge(w_lo_ready, met)
                    load_expert(e)

            slots_of(sp, pro, slot, last)
            sp.wait_ge(adds_out, NE * NBLK * JT * 16)
            sp.wait_ge(y_out, B * 16)

        @block.gpsimd
        def _(pool):
            pool.memset(ident[:, :], 0.0).then_inc(const_step, 1)
            pool.memset(before[:, :], 1.0).then_inc(const_step, 1)
            pool.wait_ge(const_step, 2)
            pool.affine_select(out=ident[:, :], in_=ident[:, :], compare_op=ALU.not_equal, fill=1.0, base=0,
                               pattern=[[-1, P]], channel_multiplier=1).then_inc(ident_ready, 1)
            pool.affine_select(out=before[:, :], in_=before[:, :], compare_op=ALU.is_gt, fill=0.0, base=0,
                               pattern=[[1, P]], channel_multiplier=-1).then_inc(const_ready, 1)
            pool.memset(ones[:, :], 1.0).then_inc(const_ready, 1)
            pool.memset(minus_half[:, :], -0.5).then_inc(const_ready, 1)
            pool.iota(expert_no_i[:, :], pattern=[[1, NE]], base=0, channel_multiplier=0).then_inc(const_ready, 1)
            pool.iota(token_no[:, :], pattern=[[P, C]], base=0, channel_multiplier=1).then_inc(const_ready, 1)
            for p in (0, 1):
                pool.memset(vaug[p][:, :, :, :], 0.0).then_inc(const_step, 1)
                pool.memset(xe[p][:, :, :], 0.0).then_inc(xe_zero, 1)
            pool.memset(empty[:, :, 0], T).then_inc(const_ready, 1)
            pool.memset(empty[:, :, 1], 0).then_inc(const_ready, 1)
            pool.wait_ge(const_step, 4)
            for p in (0, 1):
                pool.memset(vaug[p][:, :, :, HD:HD + 1], 1.0).then_inc(const_ready, 1)
            pool.wait_ge(const_ready, CONSTANTS)
            for p in (0, 1):
                pool.memset(qst[p][KS:P, :, :], 0.0).then_inc(rows_ready, 1)
            pool.wait_ge(rows_ready, 2)
            pool.dma_start(slots.rearrange("(p n) w -> p (n w)", p=P), empty[:, :, :].rearrange("p n w -> p (n w)"))\
                .then_inc(table_empty, 16)

            pool.wait_ge(table_empty, 16)
            for n in range(3):
                pool.wait_ge(wT_hi_ready, n + 1)
                pool.tensor_tensor(wT_lo[n][:, :, :], wT[n][:, :, :], wT_hi[n][:, :, :], ALU.subtract)\
                    .then_inc(wT_lo_ready, 1)

            def scale_x(t, p):
                pool.wait_ge(x_in[p], (t * 16 + (32 - 16 * p)).value)
                pool.wait_ge(xn_ready, (t * 2).value)
                pool.tensor_tensor(xs[:, :, :], x_tok[p][:, :, :],
                                   s1_all[p][:, :].unsqueeze(1).to_broadcast([P, C, D]), ALU.mult)\
                    .then_inc(xs_ready, 1)

            def inverse_root(t):
                pool.wait_ge(var_ready, (t + 1).value)
                pool.tensor_tensor(rstd[:, :], var[:, :], minus_half[:, 0:C], ALU.pow).then_inc(rstd_ready, 1)

            def small_parts(t, use, parts, rest, second, third):
                met = ahead(pool, uses(use, t))
                pool.wait_ge(const_ready, CONSTANTS)
                pool.wait_ge(drained[BANK[use]], met)
                pool.tensor_copy(parts[:, :, 1, :], rest[:, :, :]).then_inc(second, 1)
                pool.wait_ge(second, (t + 1).value)
                pool.tensor_tensor(parts[:, :, 2, :], rest[:, :, :], parts[:, :, 1, :], ALU.subtract)\
                    .then_inc(third, 1)

            def split(t, p):
                small_parts(t, "q", qparts, qrest, q2_ready, q3_ready)
                small_parts(t, "k", kparts, krest, k2_ready, k3_ready)

            def enter(t, p):
                met = ahead(pool, t + 1)
                pool.wait_ge(const_ready, CONSTANTS)
                pool.wait_ge(entry_ready, met)
                for c in range(C):
                    for k in range(TOPK):
                        pool.indirect_dma_start(
                            out=slots, out_offset=bass.IndirectOffsetOnAxis(ap=slot_i[:, c, k:k + 1], axis=0),
                            in_=entry[:, c, k, :], in_offset=None, bounds_check=NE * CAP - 1, oob_is_err=False)\
                            .then_inc(entries_out, 16)

            def pro():
                for t, p in ((Count(0), 0), (Count(1), 1)):
                    scale_x(t, p)
                    inverse_root(t)
                for t, p in ((Count(0), 0), (Count(1), 1)):
                    split(t, p)
                scale_x(Count(2), 0)
                inverse_root(Count(2))

            def slot(s, p):
                if has(s, 2):
                    split(s + 2, p)
                if has(s, 3):
                    scale_x(s + 3, 1 - p)
                if has(s, 3):
                    inverse_root(s + 3)
                if has(s, -1):
                    enter(s - 1, 1 - p)

            def fetch(nb, b):
                pool.dma_start(tab[b][:, :, :], slots[bass.ds((nb * BLK).value, BLK), :].rearrange("(p j) w -> p j w", j=JT))\
                    .then_inc(tab_in, 16)
                met = ahead(pool, nb * 16 + 16)
                pool.wait_ge(const_ready, CONSTANTS)
                pool.wait_ge(tab_in, met)
                for j in range(JT):
                    pool.indirect_dma_start(
                        out=xe[b][:, j, :], out_offset=None, in_=y_rows,
                        in_offset=bass.IndirectOffsetOnAxis(ap=tab[b][:, j, 0:1].bitcast(U32), axis=0),
                        bounds_check=T - 1, oob_is_err=False).then_inc(xe_in[b], 16)

            def add(nb, b):
                met = ahead(pool, nb + 1)
                pool.wait_ge(const_ready, CONSTANTS)
                pool.wait_ge(ye_act, met)
                pool.wait_ge(ye_dve, (nb + 1).value)
                for j in range(JT):
                    pool.indirect_dma_start(
                        out=out_rows, out_offset=bass.IndirectOffsetOnAxis(ap=tab[b][:, j, 0:1].bitcast(U32), axis=0),
                        in_=ye[:, j, :], in_offset=None, bounds_check=T - 1, oob_is_err=False,
                        compute_op=ALU.add).then_inc(adds_out, 16)

            def last():
                pool.wait_ge(entries_out, B * C * TOPK * 16)
                pool.wait_ge(y_out, B * 16)
                pool.wait_ge(xe_zero, 2)
                pool.wait_ge(out_is_x, B * 16)
                fetch(Count(0), 0)

                def blocks(i, more):
                    for j in range(2 * NBLK):
                        if more or j < 2 * NBLK - 1:
                            fetch(at(i, j + 1), (j + 1) % 2)
                        add(at(i, j), j % 2)
                        met = ahead(pool, (at(i, j) + 1) * (JT * 16))
                        pool.wait_ge(const_ready, CONSTANTS)
                        pool.wait_ge(adds_out, met)

                with pool.Fori(0, NE // 2 - 1) as i:
                    blocks(i, True)
                blocks(NE // 2 - 1, False)

            slots_of(pool, pro, slot, last)

        @block.scalar
        def _(act):
            for n in range(3):
                act.wait_ge(set_drained, n + 2)
                act.activation(wT_hi[n][:, :, :], wT[n][:, :, :], ACT.Copy).then_inc(wT_hi_ready, 1)
            act.wait_ge(set_drained, 11)
            act.activation(dcoef_all[:, :, :, :], dsum[:, :, :, :], ACT.Sqrt).then_inc(roots_ready, 1)
            act.wait_ge(d_ready, 3)

            def ev_xT(t, p):
                b = BANK["xT"]
                act.wait_ge(filled[b], uses("xT", t).value)
                act.activation(xT_hi[:, :, :], gen3[b], ACT.Copy).then_inc(xT_hi_ready, 1)

            def first_part(t, p, use, n, parts, first):
                b = BANK[use]
                act.wait_ge(filled[b], uses(use, t).value)
                for c in range(C):
                    ins = act.activation(parts[:, c, 0, :], gen3[b][:, c, :], ACT.Copy,
                                         scale=dcoef[n][:, c, bass.ds(t.value, 1)])
                ins.then_inc(first, 1)

            def parts_free(t, n):
                act.wait_ge(parts_out[n], (t * 16).value)

            def ev_vT(t, p):
                b = BANK["vT"]
                act.wait_ge(filled[b], uses("vT", t).value)
                for c in range(C):
                    ins = act.activation(vT[p][:, c, :], gen3[b][:, c, :], ACT.Copy,
                                         scale=dcoef[WV][:, c, bass.ds(t.value, 1)])
                ins.then_inc(drained[b], 1)

            def ev_v(t, p):
                b = BANK["v"]
                act.wait_ge(av_done, ((t - 1) * 4).value)
                act.wait_ge(filled[b], uses("v", t).value)
                for c in range(C):
                    ins = act.activation(vaug[p][:, c, :, 0:HD], gen3[b][:, c, :].rearrange("p (h d) -> p h d", d=HD),
                                         ACT.Copy)
                ins.then_inc(drained[b], 1)

            def exps(t, p, h):
                if h in (8, 12):
                    act.wait_ge(av_done, (t * 4 + (h // 4 - 1)).value)
                act.wait_ge(t_filled, (t * H + (h + 1)).value)
                act.activation(probs[h % 8][:, :, :], st_ps[h % 2][:, :].rearrange("p (c q) -> p c q", c=C),
                               ACT.Exp).then_inc(p_ready, 1)

            def ev_o(t, p, n):
                act.wait_ge(av_done, (t * 4 + (2 * n + 2)).value)
                act.activation(oTa[:, 2 * n:2 * n + 2, :], o_ps[n][:, :].rearrange("p (g q) -> p g q", g=2), ACT.Copy)\
                    .then_inc(o_drained, 1)

            def ev_oT(t, p):
                b = BANK["oT"]
                act.wait_ge(filled[b], uses("oT", t).value)
                act.activation(oT[:, :, :], gen3[b], ACT.Copy).then_inc(drained[b], 1)

            def ev_u(t, p):
                b = BANK["u"]
                act.wait_ge(filled[b], uses("u", t).value)
                for c in range(C):
                    ins = act.activation(skipT[:, c, :], gen3[b][:, c, :], ACT.Copy,
                                         scale=dcoef[WU][:, c, bass.ds(t.value, 1)])
                ins.then_inc(drained[b], 1)

            def ev_y(t, p):
                b = BANK["y"]
                act.wait_ge(y_out, (t * 16).value)
                act.wait_ge(filled[b], uses("y", t).value)
                act.activation(y_tok[:, :, :], gen3[b], ACT.Copy).then_inc(drained[b], 1)

            def ex_gap(t, p):
                act.wait_ge(gap_ready, (t + 1).value)
                act.wait_ge(pr_ready, t.value)
                act.activation(ex[:, :], gap[:, :], ACT.Exp).then_inc(ex_ready, 1)

            def pro():
                for t, p in ((Count(0), 0), (Count(1), 1)):
                    ev_xT(t, p)
                    parts_free(t, 0)
                    first_part(t, p, "q", WQ, qparts, q1_ready)
                    parts_free(t, 1)
                    first_part(t, p, "k", WK, kparts, k1_ready)
                    ev_vT(t, p)
                    if p == 0:
                        ev_v(t, p)

            def split_high(e, p, n):
                act.wait_ge(w_raw_in, (e * 48 + 48).value)
                act.activation(piece(w_hi[p], n), piece(w_raw, n), ACT.Copy).then_inc(w_hi_ready, 1)

            def take_high(nb):
                act.wait_ge(up_filled, (nb * FC).value)
                for c in range(C):
                    act.wait_ge(xeT_filled, (nb * C + (c + 1)).value)
                    act.activation(xeT_hi[:, c, :], gen[c][:, :], ACT.Copy).then_inc(xeT_hi_ready, 1)

            def hidden_high(nb, f):
                act.wait_ge(h_ready, (nb * FC + (f + 1)).value)
                act.activation(hid_hi[:, f, :], hid[f % 2][:, :], ACT.Copy).then_inc(h_hi_ready, 1)

            def slot(s, p):
                for i in range(H + LAG):
                    if i >= LAG and has(s, 0):
                        exps(s, p, i - LAG)
                    if i == 1 and has(s, -1):
                        ev_o(s - 1, 1 - p, 1)
                    if i == 1 and has(s, 2):
                        ev_xT(s + 2, p)
                    if i == 4 and has(s, 2):
                        parts_free(s + 2, 0)
                        first_part(s + 2, p, "q", WQ, qparts, q1_ready)
                    if i == 5 and has(s, 2):
                        parts_free(s + 2, 1)
                        first_part(s + 2, p, "k", WK, kparts, k1_ready)
                    if i == 6 and has(s, -1):
                        ev_oT(s - 1, 1 - p)
                    if i == 11 and has(s, -1):
                        ev_y(s - 1, 1 - p)
                    if i == 12 and has(s, 0):
                        ev_u(s, p)
                    if i == 13 and has(s, -1):
                        ex_gap(s - 1, 1 - p)
                    if i == 15 and has(s, 1):
                        ev_v(s + 1, 1 - p)
                    if i == 18 and has(s, 0):
                        ev_o(s, p, 0)
                    if i == 19 and has(s, 2):
                        ev_vT(s + 2, p)
                for n in range(PIECES):
                    if s.i is None and s.first == B - 2 + n // 2:
                        split_high(Count(0), 0, n)

            def blocks(i, more):
                for j in range(2 * NBLK):
                    nb = at(i, j)
                    for f in range(FC):
                        act.wait_ge(up_filled, (nb * FC + (f + 1)).value)
                        act.activation(sg[f % 2][:, :], banks[2 + f % 2][:, :], ACT.Silu).then_inc(sg_ready, 1)
                        if f >= 1:
                            hidden_high(nb, f - 1)
                    hidden_high(nb, FC - 1)
                    if more or j < 2 * NBLK - 1:
                        take_high(nb + 1)
                    e, these = pieces_at(i, j)
                    for n in these:
                        split_high(e, 1 - j // NBLK, n)
                    act.wait_ge(down_filled, (nb * 2 + 2).value)
                    if last_one(i, j):
                        act.wait_ge(adds_out, (nb * (JT * 16)).value)
                    for tt in (2, 3):
                        ins = act.activation(ye[:, tt, :], o_ps[1][:, (tt - 2) * D:(tt - 1) * D], ACT.Copy,
                                             scale=tab[j % 2][:, tt, 1:2].bitcast(F32))
                    ins.then_inc(ye_act, 1)

            def last():
                take_high(Count(0))
                with act.Fori(0, NE // 2 - 1) as i:
                    blocks(i, True)
                blocks(NE // 2 - 1, False)

            slots_of(act, pro, slot, last)

        @block.vector
        def _(dve):
            for p in (0, 1):
                dve.memset(kst[p][KS:P, :, :], 0.0).then_inc(rows_zero, 1)
            dve.wait_ge(const_ready, CONSTANTS)
            dve.tensor_copy(expert_no[:, :], expert_no_i[:, :]).then_inc(numbers_ready, 1)
            dve.tensor_copy(token_f[:, :], token_no[:, :]).then_inc(numbers_ready, 1)
            dve.memset(base[:, 0, :], 0.0).then_inc(base_step, 1)
            dve.wait_ge(numbers_ready, 2)
            dve.tensor_scalar(expert_base[:, :], expert_no[:, :], float(CAP), None, ALU.mult).then_inc(d_ready, 1)
            dve.wait_ge(set_filled, 1)
            dve.tensor_copy(condT[:, :, :], banks[2][:, 0:4 * B].rearrange("p (c b) -> p c b", c=4))\
                .then_inc(set_drained, 1)
            dve.wait_ge(set_drained, 1)
            dve.tensor_tensor(condsq[:, :, :], condT[:, :, :], condT[:, :, :], ALU.mult).then_inc(sq_ready, 1)
            for n in range(5):
                dve.wait_ge(set_filled, n + 2)
                src = banks[2 + (n + 1) % 2][:, :].rearrange("p (c o) -> p c o", c=C)
                for c in range(C):
                    if n in (WQ, WK):
                        dst = wT[n][:, c, :].rearrange("p (k d h) -> p k h d", k=C, d=HD)
                        ins = dve.tensor_copy(dst, src[:, c, :].rearrange("p (k h d) -> p k h d", k=C, d=HD))
                    else:
                        ins = dve.tensor_copy(wT[n][:, c, :], src[:, c, :])
                ins.then_inc(set_drained, 1)
                dve.wait_ge(set_drained, n + 2)
                dve.tensor_tensor(squares[n][:, :, :], wT[n][:, :, :], wT[n][:, :, :], ALU.mult).then_inc(sq_ready, 1)
            for n in range(5):
                dve.wait_ge(set_filled, n + 7)
                ps = banks[2 + n % 2][:, 0:C * B].rearrange("p (c b) -> p c b", c=C)
                dve.tensor_scalar(dsum[:, n, :, :], ps, 1e-8, None, ALU.add).then_inc(set_drained, 1)
            dve.wait_ge(roots_ready, 1)
            dve.reciprocal(dcoef_all[:, :, :, :], dcoef_all[:, :, :, :]).then_inc(newton_step, 1)
            dve.wait_ge(newton_step, 1)
            dve.tensor_tensor(dwork[:, :, :, :], dcoef_all[:, :, :, :], dcoef_all[:, :, :, :], ALU.mult)\
                .then_inc(newton_step, 1)
            dve.wait_ge(newton_step, 2)
            dve.tensor_tensor(dwork[:, :, :, :], dwork[:, :, :, :], dsum[:, :, :, :], ALU.mult).then_inc(newton_step, 1)
            dve.wait_ge(newton_step, 3)
            dve.tensor_scalar(dwork[:, :, :, :], dwork[:, :, :, :], -0.5, 1.5, ALU.mult, ALU.add)\
                .then_inc(newton_step, 1)
            dve.wait_ge(newton_step, 4)
            dve.tensor_tensor(dcoef_all[:, :, :, :], dcoef_all[:, :, :, :], dwork[:, :, :, :], ALU.mult)\
                .then_inc(newton_step, 1)
            dve.wait_ge(newton_step, 5)
            dve.tensor_scalar(dcoef[WQ][:, :, :], dcoef[WQ][:, :, :], HD ** -0.5, None, ALU.mult).then_inc(d_ready, 1)
            dve.tensor_tensor(dcoef[WV][:, :, :], dcoef[WV][:, :, :], condT[:, C:2 * C, :], ALU.mult)\
                .then_inc(d_ready, 1)
            dve.wait_ge(d_ready, 3)

            def norm_stats(t, p):
                dve.wait_ge(xs_ready, (t + 1).value)
                for c in range(C):
                    ins = dve.bn_stats(stats[:, c, :], xs[:, c, :])
                ins.then_inc(stats_ready, 1)

            def norm_var(t, p):
                met = ahead(dve, t + 1)
                dve.wait_ge(const_ready, CONSTANTS)
                dve.wait_ge(stats_ready, met)
                for c in range(C):
                    ins = dve.bn_aggr(mv[:, c, :], stats[:, c, :])
                ins.then_inc(aggr_ready, 1)
                dve.wait_ge(aggr_ready, (t + 1).value)
                dve.tensor_scalar(var[:, :], mv[:, :, 1], 1e-5, None, ALU.add).then_inc(var_ready, 1)

            def norm_x(t, p):
                dve.wait_ge(rstd_ready, (t + 1).value)
                dve.tensor_scalar(xn[:, 0, :], xs[:, 0, :], mv[:, 0, 0:1], rstd[:, 0:1], ALU.subtract, ALU.mult)\
                    .then_inc(xn_ready, 1)

            def norm_x_rest(t, p):
                dve.tensor_scalar(xn[:, 1, :], xs[:, 1, :], mv[:, 1, 0:1], rstd[:, 1:2], ALU.subtract, ALU.mult)\
                    .then_inc(xn_ready, 1)

            def norm(t, p):
                norm_stats(t, p)
                norm_var(t, p)
                norm_x(t, p)
                norm_x_rest(t, p)

            def ev_xT_low(t, p):
                b = BANK["xT"]
                dve.wait_ge(xT_hi_ready, (t + 1).value)
                dve.tensor_tensor(xT_lo[:, :, :], gen3[b], xT_hi[:, :, :], ALU.subtract).then_inc(drained[b], 1)

            def rest(t, p, use, n, parts, rst, first, third):
                b = BANK[use]
                dve.wait_ge(first, (t + 1).value)
                dve.wait_ge(third, t.value)
                for c in range(C):
                    ins = dve.scalar_tensor_tensor(out=rst[:, c, :], in0=gen3[b][:, c, :],
                                                   scalar=dcoef[n][:, c, bass.ds(t.value, 1)], in1=parts[:, c, 0, :],
                                                   op0=ALU.mult, op1=ALU.subtract)
                ins.then_inc(drained[b], 1)

            def maxima(t, p, h):
                dve.wait_ge(s_filled, (t * H + (h + 1)).value)
                dve.tensor_reduce(mx[:, :, h], sc_ps[h % 2][:, :].rearrange("p (c k) -> p c k", c=C), AX.X, ALU.max)\
                    .then_inc(s_drained, 1)

            def minus_max(t, p):
                b = BANK["maxT"]
                ps = gen[b][0:H, 0:S]
                dve.wait_ge(nm_in, (t * 48).value)
                dve.wait_ge(filled[b], uses("maxT", t).value)
                dve.tensor_scalar(nm[:, 0, :], ps, -1.0, None, ALU.mult).then_inc(n1_ready, 1)

            def minus_max_rest(t, p):
                b = BANK["maxT"]
                ps = gen[b][0:H, 0:S]
                dve.wait_ge(n1_ready, (t + 1).value)
                dve.scalar_tensor_tensor(out=nrest[:, :], in0=ps, scalar=-1.0, in1=nm[:, 0, :],
                                         op0=ALU.mult, op1=ALU.subtract).then_inc(drained[b], 1)

            def minus_max_small(t, p):
                dve.wait_ge(drained[BANK["maxT"]], uses("maxT", t).value)
                dve.tensor_copy(nm[:, 1, :], nrest[:, :]).then_inc(n2_ready, 1)
                dve.wait_ge(n2_ready, (t + 1).value)
                dve.tensor_tensor(nm[:, 2, :], nrest[:, :], nm[:, 1, :], ALU.subtract).then_inc(n3_ready, 1)

            def normalise(t, p, c):
                use = ("o2a", "o2b")[c]
                b = BANK[use]
                ps = gen[b][:, :].rearrange("p (h w) -> p h w", w=VW)
                dve.wait_ge(filled[b], uses(use, t).value)
                dve.reciprocal(rden[:, c, :], ps[:, :, HD]).then_inc(rden_ready, 1)
                dve.wait_ge(rden_ready, (t * 2 + (c + 1)).value)
                dve.tensor_tensor(on[:, c, :].rearrange("p (h d) -> p h d", d=HD), ps[:, :, 0:HD],
                                  rden[:, c, :].unsqueeze(2).to_broadcast([P, H, HD]), ALU.mult)\
                    .then_inc(drained[b], 1)

            def ev_w(t, p):
                b = BANK["w"]
                dve.wait_ge(filled[b], uses("w", t).value)
                dve.wait_ge(drained[BANK["u"]], uses("u", t).value)
                for c in range(C):
                    ins = dve.scalar_tensor_tensor(out=yT[:, c, :], in0=gen3[b][:, c, :],
                                                   scalar=dcoef[WW][:, c, bass.ds(t.value, 1)], in1=skipT[:, c, :],
                                                   op0=ALU.mult, op1=ALU.add)
                ins.then_inc(drained[b], 1)

            def choose(t, p):
                b = BANK["lg"]
                dve.wait_ge(filled[b], uses("lg", t).value)
                dve.tensor_scalar(lg[:, :, :], gen[b][:, 0:C * NE].rearrange("p (c e) -> p c e", c=C), CLAMP, -CLAMP,
                                  ALU.min, ALU.max).then_inc(drained[b], 1)

            def choose_top(t, p):
                b = BANK["lg"]
                met = ahead(dve, uses("lg", t))
                dve.wait_ge(const_ready, CONSTANTS)
                dve.wait_ge(drained[b], met)
                for c in range(C):
                    ins = dve.max(top8[:, c, :], lg[:, c, :])
                ins.then_inc(top_ready, 1)

            def choose_index(t, p):
                met = ahead(dve, t + 1)
                dve.wait_ge(const_ready, CONSTANTS)
                dve.wait_ge(top_ready, met)
                for c in range(C):
                    ins = dve.max_index(idx8[:, c, :], top8[:, c, :], lg[:, c, :])
                ins.then_inc(idx_ready, 1)
                dve.wait_ge(ex_ready, t.value)
                dve.tensor_tensor(gap[:, :], top8[:, :, 1], top8[:, :, 0], ALU.subtract).then_inc(gap_ready, 1)

            def choose_number(t, p):
                dve.wait_ge(idx_ready, (t + 1).value)
                dve.tensor_copy(idxf[:, :, :], idx8[:, :, 0:TOPK]).then_inc(idxf_ready, 1)

            def choose_onehot(t, p):
                dve.wait_ge(idxf_ready, (t + 1).value)
                for k in range(TOPK):
                    dve.tensor_tensor(onehot[:, :, k, :], expert_no[:, :].unsqueeze(1).to_broadcast([P, C, NE]),
                                      idxf[:, :, k:k + 1].to_broadcast([P, C, NE]), ALU.is_equal)\
                        .then_inc(onehot_ready, 1)

            def choose_sum(t, p):
                dve.wait_ge(onehot_ready, (t * 2 + 2).value)
                dve.tensor_tensor(chosen[:, :, :], onehot[:, :, 0, :], onehot[:, :, 1, :], ALU.add)\
                    .then_inc(chosen_ready, 1)

            def weigh(t, p):
                dve.wait_ge(ex_ready, (t + 1).value)
                dve.tensor_scalar(den[:, :], ex[:, :], 1.0, 1e-12, ALU.add, ALU.add).then_inc(den_ready, 1)

            def weigh_first(t, p):
                dve.wait_ge(den_ready, (t * 2 + 1).value)
                dve.reciprocal(pr[:, :, 0], den[:, :]).then_inc(den_ready, 1)

            def weigh_second(t, p):
                dve.wait_ge(den_ready, (t * 2 + 2).value)
                dve.tensor_tensor(pr[:, :, 1], ex[:, :], pr[:, :, 0], ALU.mult).then_inc(pr_ready, 1)

            def route(t, p):
                b = BANK["rt"]
                dve.wait_ge(filled[b], uses("rt", t).value)
                ps = gen[b]
                for c in range(C):
                    dve.wait_ge(base_step, (t * 3 + (c + 1)).value)
                    dve.tensor_tensor(base[:, c + 1, :], base[:, c, :], ps[:, (C + c) * NE:(C + c + 1) * NE], ALU.add)\
                        .then_inc(base_step, 1)
                dve.tensor_tensor(pos[:, :, :], ps[:, 0:C * NE].rearrange("p (c e) -> p c e", c=C), base[:, 0:C, :],
                                  ALU.add).then_inc(drained[b], 1)

            def route_place(t, p):
                b = BANK["rt"]
                dve.wait_ge(drained[b], uses("rt", t).value)
                dve.wait_ge(base_step, (t * 3 + 3).value)
                dve.tensor_copy(base[:, 0, :], base[:, C, :]).then_inc(base_step, 1)
                dve.tensor_scalar(over[:, :, :], pos[:, :, :], float(CAP), FAR, ALU.is_ge, ALU.mult)\
                    .then_inc(over_ready, 1)
                dve.tensor_tensor(place[:, :, :], pos[:, :, :], expert_base[:, :].unsqueeze(1).to_broadcast([P, C, NE]),
                                  ALU.add).then_inc(place_step, 1)

            def route_slot(t, p):
                dve.wait_ge(over_ready, (t + 1).value)
                dve.wait_ge(place_step, (t * 2 + 1).value)
                dve.tensor_tensor(place[:, :, :], place[:, :, :], over[:, :, :], ALU.add).then_inc(place_step, 1)
                dve.wait_ge(place_step, (t * 2 + 2).value)
                for k in range(TOPK):
                    ins = dve.tensor_tensor(picked[:, :, k, :], onehot[:, :, k, :], place[:, :, :], ALU.mult)
                ins.then_inc(picked_ready, 1)
                dve.wait_ge(picked_ready, (t + 1).value)
                dve.tensor_reduce(slot_f[:, :, :], picked[:, :, :, :], AX.X, ALU.add).then_inc(slotf_ready, 1)
                dve.wait_ge(slotf_ready, (t + 1).value)
                dve.wait_ge(entries_out, (t * (C * TOPK * 16)).value)
                dve.tensor_copy(slot_i[:, :, :], slot_f[:, :, :])
                dve.tensor_copy(entry[:, :, :, 0], token_f[:, :].unsqueeze(2).to_broadcast([P, C, TOPK]))\
                    .then_inc(token_read, 1)
                dve.wait_ge(pr_ready, (t + 1).value)
                dve.tensor_copy(entry[:, :, :, 1].bitcast(F32), pr[:, :, :]).then_inc(entry_ready, 1)
                dve.wait_ge(token_read, (t * 2 + 1).value)
                dve.tensor_scalar(token_f[:, :], token_f[:, :], float(S), None, ALU.add).then_inc(token_read, 1)
                dve.wait_ge(token_read, (t * 2 + 2).value)

            def pro():
                norm(Count(0), 0)
                ev_xT_low(Count(0), 0)
                norm_stats(Count(1), 1)
                norm_var(Count(1), 1)
                norm_x(Count(1), 1)
                norm_x_rest(Count(1), 1)
                rest(Count(0), 0, "q", WQ, qparts, qrest, q1_ready, q3_ready)
                rest(Count(0), 0, "k", WK, kparts, krest, k1_ready, k3_ready)
                dve.wait_ge(rows_zero, 2)
                for p in (0, 1):
                    dve.memset(kst[p][KS:KM, :, :].rearrange("r h s -> r (h s)").bitcast(F32), TWO_ONES)\
                        .then_inc(rows_ready, 1)
                ev_xT_low(Count(1), 1)
                rest(Count(1), 1, "q", WQ, qparts, qrest, q1_ready, q3_ready)
                rest(Count(1), 1, "k", WK, kparts, krest, k1_ready, k3_ready)
                for h in range(H):
                    maxima(Count(0), 0, h)
                minus_max(Count(0), 0)
                minus_max_rest(Count(0), 0)
                minus_max_small(Count(0), 0)
                norm(Count(2), 0)

            def slot(s, p):
                for i in range(H + LAG):
                    if i < H and has(s, 1):
                        maxima(s + 1, 1 - p, i)
                    if i == 1 and has(s, 2):
                        ev_xT_low(s + 2, p)
                    if i == 2 and has(s, -1):
                        normalise(s - 1, 1 - p, 0)
                    if i == 3 and has(s, -1):
                        normalise(s - 1, 1 - p, 1)
                    if i == 5 and has(s, 2):
                        rest(s + 2, p, "q", WQ, qparts, qrest, q1_ready, q3_ready)
                    if i == 6 and has(s, 2):
                        rest(s + 2, p, "k", WK, kparts, krest, k1_ready, k3_ready)
                    if i == 8 and has(s, -1):
                        ev_w(s - 1, 1 - p)
                    if i == 10 and has(s, -1):
                        choose(s - 1, 1 - p)
                    if i == 11 and has(s, -1):
                        choose_top(s - 1, 1 - p)
                    if i == 12 and has(s, 3):
                        norm_stats(s + 3, 1 - p)
                    if i == 12 and has(s, -1):
                        choose_index(s - 1, 1 - p)
                    if i == 13 and has(s, -1):
                        choose_number(s - 1, 1 - p)
                    if i == 13 and has(s, 3):
                        norm_var(s + 3, 1 - p)
                    if i == 15 and has(s, -1):
                        choose_onehot(s - 1, 1 - p)
                    if i == 15 and has(s, 1):
                        minus_max(s + 1, 1 - p)
                    if i == 15 and has(s, -1):
                        choose_sum(s - 1, 1 - p)
                        weigh(s - 1, 1 - p)
                    if i == 15 and has(s, 1):
                        minus_max_rest(s + 1, 1 - p)
                    if i == 15 and has(s, -1):
                        weigh_first(s - 1, 1 - p)
                    if i == 15 and has(s, 1):
                        minus_max_small(s + 1, 1 - p)
                    if i == 16 and has(s, -1):
                        weigh_second(s - 1, 1 - p)
                    if i == 18 and has(s, -1):
                        route(s - 1, 1 - p)
                    if i == 18 and has(s, 3):
                        norm_x(s + 3, 1 - p)
                    if i == 18 and has(s, -1):
                        route_place(s - 1, 1 - p)
                    if i == 18 and has(s, 3):
                        norm_x_rest(s + 3, 1 - p)
                    if i == 18 and has(s, -1):
                        route_slot(s - 1, 1 - p)
                for n in range(PIECES):
                    if s.i is None and s.first == B - 2 + n // 2:
                        split_low(Count(0), 0, n)

            def split_low(e, p, n):
                dve.wait_ge(w_hi_ready, (e * PIECES + (n + 1)).value)
                dve.tensor_tensor(piece(w_lo[p], n), piece(w_raw, n), piece(w_hi[p], n), ALU.subtract)\
                    .then_inc(w_lo_ready, 1)

            def take_low(nb):
                for c in range(C):
                    dve.wait_ge(xeT_hi_ready, (nb * C + (c + 1)).value)
                    dve.tensor_tensor(xeT_lo[:, c, :], gen[c][:, :], xeT_hi[:, c, :], ALU.subtract)\
                        .then_inc(xeT_lo_ready, 1)

            def hidden_low(nb, f):
                dve.wait_ge(h_hi_ready, (nb * FC + (f + 1)).value)
                dve.tensor_tensor(hid_lo[:, f, :], hid[f % 2][:, :], hid_hi[:, f, :], ALU.subtract)\
                    .then_inc(h_lo_ready, 1)

            def blocks(i, more):
                for j in range(2 * NBLK):
                    nb = at(i, j)
                    for f in range(FC):
                        dve.wait_ge(sg_ready, (nb * FC + (f + 1)).value)
                        if f >= 2:
                            dve.wait_ge(h_lo_ready, (nb * FC + (f - 1)).value)
                        dve.tensor_tensor(hid[f % 2][:, :], sg[f % 2][:, :], banks[4 + f % 2][:, :], ALU.mult)\
                            .then_inc(h_ready, 1)
                        if f >= 1:
                            hidden_low(nb, f - 1)
                    hidden_low(nb, FC - 1)
                    if more or j < 2 * NBLK - 1:
                        take_low(nb + 1)
                    e, these = pieces_at(i, j)
                    for n in these:
                        split_low(e, 1 - j // NBLK, n)
                    dve.wait_ge(down_filled, (nb * 2 + 1).value)
                    if last_one(i, j):
                        dve.wait_ge(adds_out, (nb * (JT * 16)).value)
                    for tt in (0, 1):
                        ins = dve.tensor_scalar(ye[:, tt, :], o_ps[0][:, tt * D:(tt + 1) * D],
                                                tab[j % 2][:, tt, 1:2].bitcast(F32), None, ALU.mult)
                    ins.then_inc(ye_dve, 1)

            def last():
                take_low(Count(0))
                with dve.Fori(0, NE // 2 - 1) as i:
                    blocks(i, True)
                blocks(NE // 2 - 1, False)

            slots_of(dve, pro, slot, last)

        @block.tensor
        def _(pe):
            pe.wait_ge(ident_ready, 1)
            pe.wait_ge(small_in, 32)
            for c in range(4):
                ins = pe.transpose(banks[2][:, c * B:(c + 1) * B], cond_sb[:, c * P:(c + 1) * P], ident[0:B, 0:B])
            ins.then_inc(set_filled, 1)
            pe.wait_ge(w_in, 5 * 16)
            for n in range(5):
                pe.wait_ge(set_drained, n)
                for ic in range(C):
                    for oc in range(C):
                        ins = pe.transpose(banks[2 + (n + 1) % 2][:, ic * D + oc * P:ic * D + (oc + 1) * P],
                                           wload[n][:, oc, ic * P:(ic + 1) * P], ident[:, :])
                ins.then_inc(set_filled, 1)
            for n in range(5):
                pe.wait_ge(set_drained, n + 5)
                pe.wait_ge(sq_ready, n + 2)
                side = 0 if n < 3 else C
                for oc in range(C):
                    for ic in range(C):
                        ins = pe.matmul(banks[2 + n % 2][:, oc * B:(oc + 1) * B], squares[n][:, ic, oc * P:(oc + 1) * P],
                                        condsq[:, side + ic, :], start=(ic == 0), stop=(ic == C - 1))
                ins.then_inc(set_filled, 1)

            def begin(use, t):
                b = BANK[use]
                pe.wait_ge(drained[b], (uses(use, t) - 1).value)
                return b

            def transposes(dst, src):
                for a in range(C):
                    for c in range(C):
                        ins = pe.transpose(dst[:, a, c * P:(c + 1) * P], src[:, c, a * P:(a + 1) * P], ident[:, :])
                return ins

            def halves(dst, st_hi, st_lo, mv_hi, mv_lo, start, stop):
                pe.matmul(dst, st_lo, mv_hi, start=start, stop=False)
                pe.matmul(dst, st_hi, mv_lo, start=False, stop=False)
                return pe.matmul(dst, st_hi, mv_hi, start=False, stop=stop)

            def project(b, w, src):
                for m in range(C):
                    for k in range(C):
                        ins = pe.matmul(gen3[b][:, m, :], w[:, k, m * P:(m + 1) * P], src[:, k, :],
                                        start=(k == 0), stop=(k == C - 1))
                ins.then_inc(filled[b], 1)

            def project_x(b, n):
                for m in range(C):
                    for k in range(C):
                        cols = slice(m * P, (m + 1) * P)
                        ins = halves(gen3[b][:, m, :], wT_hi[n][:, k, cols], wT_lo[n][:, k, cols],
                                     xT_hi[:, k, :], xT_lo[:, k, :], k == 0, k == C - 1)
                ins.then_inc(filled[b], 1)

            def a_xT(t, p):
                b = begin("xT", t)
                pe.wait_ge(xn_ready, (t * 2 + 2).value)
                transposes(gen3[b], xn).then_inc(filled[b], 1)

            def a_proj(t, p, use, n):
                pe.wait_ge(drained[BANK["xT"]], uses("xT", t).value)
                project_x(begin(use, t), n)

            def a_v(t, p):
                b = begin("v", t)
                pe.wait_ge(drained[BANK["vT"]], uses("vT", t).value)
                transposes(gen3[b], vT[p]).then_inc(filled[b], 1)

            def scores(t, p, h):
                if h % HG == 0:
                    pe.wait_ge(stack_in[h // HG][p], (t * (8 * STACK_LOADS) + (16 - 8 * p) * STACK_LOADS).value)
                pe.wait_ge(s_drained, (t * H + (h - 1)).value)
                for c in range(C):
                    ins = pe.matmul(sc_ps[h % 2][:, c * S:(c + 1) * S], qst[p][0:KS, h, c * P:(c + 1) * P],
                                    kst[p][0:KS, h, :], start=True, stop=True)
                ins.then_inc(s_filled, 1)

            def max_t(t, p):
                b = begin("maxT", t)
                pe.wait_ge(s_drained, (t * H + H).value)
                for c in range(C):
                    ins = pe.transpose(gen[b][0:H, c * P:(c + 1) * P], mx[:, c, :], ident[:, :])
                ins.then_inc(filled[b], 1)

            def shifted(t, p, h):
                if h == 0:
                    pe.wait_ge(nm_in, (t * 48 + 48).value)
                pe.wait_ge(p_ready, (t * H + (h - 1 if h >= 2 else 0)).value)
                for c in range(C):
                    ins = pe.matmul(st_ps[h % 2][:, c * S:(c + 1) * S], kst[p][:, h, c * P:(c + 1) * P],
                                    qst[p][:, h, :], start=True, stop=True)
                ins.then_inc(t_filled, 1)

            def values(t, p, g):
                if g == 0:
                    pe.wait_ge(o_drained, (t * 2).value)
                pe.wait_ge(p_ready, (t * H + (4 * g + 4)).value)
                for c in range(C):
                    for j in range(4):
                        h = 4 * g + j
                        ins = pe.matmul(o_ps[g // 2][VW * j:VW * (j + 1), (g % 2) * S:(g % 2 + 1) * S],
                                        vaug[p][:, c, h, :], probs[h % 8][:, c, :], start=(c == 0), stop=(c == C - 1),
                                        skip_group_check=True)
                ins.then_inc(av_done, 1)

            def d_o2(t, p, c):
                use = ("o2a", "o2b")[c]
                b = begin(use, t)
                pe.wait_ge(o_drained, (t * 2 + 2).value)
                for g in range(4):
                    ins = pe.transpose(gen[b][:, g * P:(g + 1) * P], oTa[:, g, c * P:(c + 1) * P], ident[:, :])
                ins.then_inc(filled[b], 1)

            def d_oT(t, p):
                b = begin("oT", t)
                pe.wait_ge(drained[BANK["o2a"]], uses("o2a", t).value)
                pe.wait_ge(drained[BANK["o2b"]], uses("o2b", t).value)
                transposes(gen3[b], on).then_inc(filled[b], 1)

            def d_w(t, p):
                b = begin("w", t)
                pe.wait_ge(drained[BANK["oT"]], uses("oT", t).value)
                project(b, ww_T, oT)

            def d_u(t, p):
                project(begin("u", t), wu_T, vT[p])

            def d_y(t, p):
                b = begin("y", t)
                pe.wait_ge(drained[BANK["w"]], uses("w", t).value)
                transposes(gen3[b], yT).then_inc(filled[b], 1)

            def d_lg(t, p):
                b = begin("lg", t)
                pe.wait_ge(drained[BANK["w"]], uses("w", t).value)
                for c in range(C):
                    for k in range(C):
                        ins = pe.matmul(gen[b][:, c * NE:(c + 1) * NE], yT[:, k, c * P:(c + 1) * P], wr_sb[:, k, :],
                                        start=(k == 0), stop=(k == C - 1))
                ins.then_inc(filled[b], 1)

            def r_counts(t, p):
                b = begin("rt", t)
                pe.wait_ge(chosen_ready, (t + 1).value)
                pe.matmul(gen[b][:, 0:C * NE], before[:, :], chosen[:, :, :].rearrange("p c e -> p (c e)"),
                          start=True, stop=True)
                pe.matmul(gen[b][:, C * NE:2 * C * NE], ones[:, :], chosen[:, :, :].rearrange("p c e -> p (c e)"),
                          start=True, stop=True).then_inc(filled[b], 1)

            def pro():
                pe.wait_ge(d_ready, 3)
                pe.wait_ge(wT_lo_ready, 3)
                for t, p in ((Count(0), 0), (Count(1), 1)):
                    a_xT(t, p)
                    a_proj(t, p, "q", WQ)
                    a_proj(t, p, "k", WK)
                    a_proj(t, p, "vT", WV)
                    if p == 0:
                        a_v(t, p)
                for h in range(H):
                    scores(Count(0), 0, h)
                max_t(Count(0), 0)

            def slot(s, p):
                for i in range(H + LAG):
                    if i < H and has(s, 1):
                        scores(s + 1, 1 - p, i)
                    if i >= LAG and has(s, 0):
                        shifted(s, p, i - LAG)
                    if i == 1 and has(s, -1):
                        values(s - 1, 1 - p, 3)
                    if i in (9, 13, 17) and has(s, 0):
                        values(s, p, (i - 9) // 4)
                    if i == 18 and has(s, 2):
                        a_proj(s + 2, p, "vT", WV)
                    if i == 1 and has(s, 2):
                        a_xT(s + 2, p)
                    if i == 2 and has(s, -1):
                        d_o2(s - 1, 1 - p, 0)
                    if i == 3 and has(s, -1):
                        d_o2(s - 1, 1 - p, 1)
                    if i == 4 and has(s, 2):
                        a_proj(s + 2, p, "q", WQ)
                    if i == 5 and has(s, 2):
                        a_proj(s + 2, p, "k", WK)
                    if i == 6 and has(s, -1):
                        d_oT(s - 1, 1 - p)
                    if i == 8 and has(s, -1):
                        d_w(s - 1, 1 - p)
                    if i == 10 and has(s, -1):
                        d_lg(s - 1, 1 - p)
                    if i == 11 and has(s, -1):
                        d_y(s - 1, 1 - p)
                    if i == 12 and has(s, 0):
                        d_u(s, p)
                    if i == 15 and has(s, 1):
                        a_v(s + 1, 1 - p)
                    if i == 16 and has(s, 1):
                        max_t(s + 1, 1 - p)
                    if i == 17 and has(s, -1):
                        r_counts(s - 1, 1 - p)

            def turn(nb, half, b):
                pe.wait_ge(xeT_lo_ready, (nb * C).value)
                pe.wait_ge(xe_in[b], ((half + 1) * (JT * 16)).value)
                for c in range(C):
                    for j in range(JT):
                        ins = pe.transpose(gen[c][:, j * P:(j + 1) * P], xe[b][:, j, c * P:(c + 1) * P], ident[:, :])
                    ins.then_inc(xeT_filled, 1)

            def up(nb, e):
                pe.wait_ge(xeT_lo_ready, (nb * C + C).value)
                for f in range(FC):
                    if f >= 2:
                        pe.wait_ge(h_ready, (nb * FC + (f - 1)).value)
                    for n, bank in ((0, banks[2 + f % 2]), (1, banks[4 + f % 2])):
                        for c in range(C):
                            at_f = c * F + f * P
                            ins = halves(bank[:, :], w_hi[e][:, n, at_f:at_f + P], w_lo[e][:, n, at_f:at_f + P],
                                         xeT_hi[:, c, :], xeT_lo[:, c, :], c == 0, c == C - 1)
                    ins.then_inc(up_filled, 1)

            def down(nb, e):
                for tt in range(JT):
                    for f in range(FC):
                        if tt == 0:
                            pe.wait_ge(h_lo_ready, (nb * FC + (f + 1)).value)
                        ins = halves(o_ps[tt // 2][:, (tt % 2) * D:(tt % 2 + 1) * D],
                                     hid_hi[:, f, tt * P:(tt + 1) * P], hid_lo[:, f, tt * P:(tt + 1) * P],
                                     w_hi[e][:, 2, f * D:(f + 1) * D], w_lo[e][:, 2, f * D:(f + 1) * D],
                                     f == 0, f == FC - 1)
                    if tt % 2:
                        ins.then_inc(down_filled, 1)

            def blocks(i, more):
                for j in range(2 * NBLK):
                    nb = at(i, j)
                    if j % NBLK == 0:
                        e = Count(2 * i + j // NBLK) if isinstance(i, int) else Count(j // NBLK, 2, i)
                        pe.wait_ge(w_lo_ready, (e * PIECES + PIECES).value)
                    up(nb, j // NBLK)
                    half = Count(i * NBLK + (j + 1) // 2) if isinstance(i, int) else Count((j + 1) // 2, NBLK, i)
                    if more or j < 2 * NBLK - 1:
                        turn(nb + 1, half, (j + 1) % 2)
                    down(nb, j // NBLK)

            def last():
                for b in (0, 1):
                    pe.wait_ge(drained[b], BANK_TOTAL[b])
                turn(Count(0), Count(0), 0)
                with pe.Fori(0, NE // 2 - 1) as i:
                    blocks(i, True)
                blocks(NE // 2 - 1, False)

            slots_of(pe, pro, slot, last)


_INS = ["x", "cond_2048", "L0_cond_q_weight", "L0_cond_k_weight", "L0_cond_v_weight", "L0_cond_w_weight",
        "L0_cond_u_weight", "L0_ffn_Wr", "L0_ffn_W1", "L0_ffn_W3", "L0_ffn_W2"]


def kernel(**inputs):
    import numpy as _np
    import concourse.bacc as _bacc
    from concourse import mybir as _mybir
    from concourse.bass_utils import run_bass_kernel_spmd as _run

    nc = _bacc.Bacc("TRN2", target_bir_lowering=False, num_devices=1)
    arrays, args = {}, []
    for name in _INS:
        a = _np.ascontiguousarray(inputs[name])
        arrays[f"in_{name}"] = a
        args.append(nc.dram_tensor(f"in_{name}", a.shape, _mybir.dt.from_np(a.dtype), kind="ExternalInput").ap())
    out = nc.dram_tensor("out_x", (B, S, D), _mybir.dt.from_np(_np.dtype("float32")), kind="ExternalOutput").ap()
    adaln_moe(nc, *args, out)
    r = _run(nc, [arrays], core_ids=[0])
    return r.results[0]["out_x"]
```
